# Optimizing a Trainium2 kernel written in Bass

```python
import numpy as np
import jax
import jax.numpy as jnp

def _softmax(x, axis=-1):
    return jax.nn.softmax(x, axis=axis)

def _gelu(x):
    return jax.nn.gelu(x, approximate=True)

def _silu(x):
    return jax.nn.silu(x)

def _sigmoid(x):
    return jax.nn.sigmoid(x)

def _layernorm(x, axis=-1, eps=1e-05):
    m = jnp.mean(x, axis=axis, keepdims=True)
    v = jnp.var(x, axis=axis, keepdims=True)
    return (x - m) / jnp.sqrt(v + eps)

def _scatter_add(tgt, idx, src, axis=0):
    return tgt.at[idx].add(src)

def _segment_sum(src, seg, n):
    return jax.ops.segment_sum(src, seg, n)
kernel_name = 'mk_decoder_preln_d1_seqx_r8_2707fd'

def setup_inputs(seed: int=0):
    np.random.seed(seed)
    _w = jnp.asarray

    def _rec_inputs():
        import jax
        import jax.numpy as jnp
        _rk = jax.random.key(seed)
        x = -0.0002928 + 1 * jax.random.normal(jax.random.fold_in(_rk, 1), (16, 128, 256), jnp.float32)
        _lenS = 128 - jax.random.randint(jax.random.fold_in(_rk, 7), (16,), 0, max(1, 128 // 4) + 1, jnp.int32)
        _lenS2 = 128 - jax.random.randint(jax.random.fold_in(_rk, 8), (16,), 0, max(1, 128 // 4) + 1, jnp.int32)
        fside_S2_0 = -0.00337071 + 1.01897 * jax.random.normal(jax.random.fold_in(_rk, 11), (128,), jnp.float32)
        _ctx_2048P = jax.random.normal(jax.random.fold_in(_rk, 12), (16, 16, 256), jnp.float32)
        _ctx_2048c = jax.random.dirichlet(jax.random.fold_in(_rk, 512), 0.3 * jnp.ones((16,), jnp.float32), (16, 128))
        _ctx_2048t = jnp.einsum('bsk,bkd->bsd', _ctx_2048c, _ctx_2048P)
        _ctx_2048t = _ctx_2048t * jax.lax.rsqrt(jnp.mean(jnp.square(_ctx_2048t)) + 1e-12) * 0.953939
        ctx_2048 = 0.000675642 + 1.00031 * (_ctx_2048t + 0.3 * jax.random.normal(jax.random.fold_in(_rk, 612), (16, 128, 256), jnp.float32))
        return (x, fside_S2_0, ctx_2048)
    x, fside_S2_0, ctx_2048 = _rec_inputs()

    def _L0_attn_setup():
        import jax, jax.numpy as jnp
        import numpy as np
        import math
        N_HEADS, D_MODEL, D_HEAD = (16, 256, 128)
        BATCH, SEQ = (4, 256)
        ROPE_THETA = 10000.0

        def _rope_cos_sin(seq_len, head_dim, dtype=jnp.float32):
            inv_freq = 1.0 / ROPE_THETA ** (jnp.arange(0, head_dim, 2, dtype=jnp.float32) / head_dim)
            m = jnp.arange(seq_len, dtype=jnp.float32)
            freqs = jnp.outer(m, inv_freq)
            return (jnp.cos(freqs).astype(dtype), jnp.sin(freqs).astype(dtype))

        def _apply_rope(x, cos, sin):
            x1 = x[..., 0::2]
            x2 = x[..., 1::2]
            cos = cos[None, :, None, :]
            sin = sin[None, :, None, :]
            r1 = x1 * cos - x2 * sin
            r2 = x1 * sin + x2 * cos
            out = jnp.stack([r1, r2], axis=-1)
            return out.reshape(x.shape)
        key = jax.random.key(seed)
        ks = jax.random.split(key, 9)
        std = 0.02
        return {'normalized_resid_pre': jax.random.normal(ks[0], (BATCH, SEQ, D_MODEL), jnp.float32), 'W_Q': jax.random.normal(ks[1], (N_HEADS, D_MODEL, D_HEAD), jnp.float32) * std, 'b_Q': jnp.zeros((N_HEADS, D_HEAD), jnp.float32), 'W_K': jax.random.normal(ks[2], (N_HEADS, D_MODEL, D_HEAD), jnp.float32) * std, 'b_K': jnp.zeros((N_HEADS, D_HEAD), jnp.float32), 'W_V': jax.random.normal(ks[3], (N_HEADS, D_MODEL, D_HEAD), jnp.float32) * std, 'b_V': jnp.zeros((N_HEADS, D_HEAD), jnp.float32), 'W_O': jax.random.normal(ks[4], (N_HEADS, D_HEAD, D_MODEL), jnp.float32) * std, 'b_O': jnp.zeros((D_MODEL,), jnp.float32)}
    _L0_attn_all = _L0_attn_setup()
    _L0_attn_in = {k: v for k, v in _L0_attn_all.items() if k in ('W_Q', 'b_Q', 'W_K', 'b_K', 'W_V', 'b_V', 'W_O', 'b_O')}
    del _L0_attn_all

    def _L0_xattn_setup():
        import jax, jax.numpy as jnp
        import numpy as np
        key = jax.random.key(seed)
        ks = jax.random.split(key, 5)
        B, D, L, NH = (2, 128, 256, 8)
        H = D // NH
        return {'v': jax.random.normal(ks[0], (B, D, L), jnp.float32), 'k': jax.random.normal(ks[1], (H, L), jnp.float32) * 0.1, 'bias': jax.random.normal(ks[2], (D,), jnp.float32), 'x1': jax.random.normal(ks[3], (B, D, L), jnp.float32), 'x2': jax.random.normal(ks[4], (B, D, L), jnp.float32), 'num_heads': NH}
    _L0_xattn_all = _L0_xattn_setup()
    _L0_xattn_in = {k: v for k, v in _L0_xattn_all.items() if k in ('k',)}
    del _L0_xattn_all

    def _L0_ffn_setup():
        import jax, jax.numpy as jnp
        import numpy as np
        B, S, H = (4, 128, 256)
        E, K, I, SI = (16, 4, 176, 704)

        def _silu_mul(gu, inter):
            return jax.nn.silu(gu[:, :inter]) * gu[:, inter:]
        key = jax.random.key(seed)
        ks = jax.random.split(key, 7)
        s = 0.02
        return {'hidden_states': jax.random.normal(ks[0], (B, S, H), jnp.float32), 'gate_w': jax.random.normal(ks[1], (E, H), jnp.float32) * s, 'expert_gate_up': jax.random.normal(ks[2], (E, 2 * I, H), jnp.float32) * s, 'expert_down': jax.random.normal(ks[3], (E, H, I), jnp.float32) * s, 'shared_gate_up': jax.random.normal(ks[4], (2 * SI, H), jnp.float32) * s, 'shared_down': jax.random.normal(ks[5], (H, SI), jnp.float32) * s, 'shared_gate_vec': jax.random.normal(ks[6], (1, H), jnp.float32) * s}
    _L0_ffn_all = _L0_ffn_setup()
    _L0_ffn_in = {k: v for k, v in _L0_ffn_all.items() if k in ('gate_w', 'expert_gate_up', 'expert_down', 'shared_gate_up', 'shared_down', 'shared_gate_vec')}
    del _L0_ffn_all
    return {'x': x, 'fside_S2_0': fside_S2_0, 'ctx_2048': ctx_2048, 'L0_attn_W_Q': _L0_attn_in['W_Q'], 'L0_attn_b_Q': _L0_attn_in['b_Q'], 'L0_attn_W_K': _L0_attn_in['W_K'], 'L0_attn_b_K': _L0_attn_in['b_K'], 'L0_attn_W_V': _L0_attn_in['W_V'], 'L0_attn_b_V': _L0_attn_in['b_V'], 'L0_attn_W_O': _L0_attn_in['W_O'], 'L0_attn_b_O': _L0_attn_in['b_O'], 'L0_xattn_k': _L0_xattn_in['k'], 'L0_ffn_gate_w': _L0_ffn_in['gate_w'], 'L0_ffn_expert_gate_up': _L0_ffn_in['expert_gate_up'], 'L0_ffn_expert_down': _L0_ffn_in['expert_down'], 'L0_ffn_shared_gate_up': _L0_ffn_in['shared_gate_up'], 'L0_ffn_shared_down': _L0_ffn_in['shared_down'], 'L0_ffn_shared_gate_vec': _L0_ffn_in['shared_gate_vec']}

def reference(x, fside_S2_0, ctx_2048, L0_attn_W_Q, L0_attn_b_Q, L0_attn_W_K, L0_attn_b_K, L0_attn_W_V, L0_attn_b_V, L0_attn_W_O, L0_attn_b_O, L0_xattn_k, L0_ffn_gate_w, L0_ffn_expert_gate_up, L0_ffn_expert_down, L0_ffn_shared_gate_up, L0_ffn_shared_down, L0_ffn_shared_gate_vec):
    import jax
    import jax.numpy as jnp

    def _L0_attn_ref(normalized_resid_pre, W_Q, b_Q, W_K, b_K, W_V, b_V, W_O, b_O):
        import jax, jax.numpy as jnp
        import numpy as np
        import math
        N_HEADS, D_MODEL, D_HEAD = (16, 256, 128)
        BATCH, SEQ = (4, 256)
        ROPE_THETA = 10000.0

        def _rope_cos_sin(seq_len, head_dim, dtype=jnp.float32):
            inv_freq = 1.0 / ROPE_THETA ** (jnp.arange(0, head_dim, 2, dtype=jnp.float32) / head_dim)
            m = jnp.arange(seq_len, dtype=jnp.float32)
            freqs = jnp.outer(m, inv_freq)
            return (jnp.cos(freqs).astype(dtype), jnp.sin(freqs).astype(dtype))

        def _apply_rope(x, cos, sin):
            x1 = x[..., 0::2]
            x2 = x[..., 1::2]
            cos = cos[None, :, None, :]
            sin = sin[None, :, None, :]
            r1 = x1 * cos - x2 * sin
            r2 = x1 * sin + x2 * cos
            out = jnp.stack([r1, r2], axis=-1)
            return out.reshape(x.shape)
        x = normalized_resid_pre
        T = x.shape[1]
        d_head = W_Q.shape[-1]
        Q = jnp.einsum('btc,ncd->btnd', x, W_Q) + b_Q
        K = jnp.einsum('btc,ncd->btnd', x, W_K) + b_K
        V = jnp.einsum('btc,ncd->btnd', x, W_V) + b_V
        cos, sin = _rope_cos_sin(T, d_head, x.dtype)
        Q = _apply_rope(Q, cos, sin)
        K = _apply_rope(K, cos, sin)
        scores = jnp.einsum('bqnd,bknd->bnqk', Q, K) / math.sqrt(d_head)
        causal = jnp.tril(jnp.ones((T, T), dtype=bool))
        scores = jnp.where(causal[None, None], scores, -jnp.inf)
        probs = jax.nn.softmax(scores, axis=-1)
        z = jnp.einsum('bnqk,bknd->bqnd', probs, V)
        out = jnp.einsum('bqnd,ndm->bqm', z, W_O) + b_O
        return out

    def _L0_xattn_ref(v, k, bias, x1, x2, num_heads):
        import jax, jax.numpy as jnp
        import numpy as np
        B, D, L = v.shape
        H = D // num_heads
        fft_size = 2 * L
        vr = v.reshape(B, H, num_heads, L)
        x1r = x1.reshape(B, H, num_heads, L)
        x2r = x2.reshape(B, H, num_heads, L)
        kv = vr[:, :, :, None, :] * x2r[:, :, None, :, :]
        k_f = jnp.fft.rfft(k.astype(jnp.float32), n=fft_size)
        y = jnp.fft.irfft(jnp.fft.rfft(kv, n=fft_size) * k_f[None, :, None, None, :], n=fft_size)[..., :L]
        skip = bias.astype(jnp.float32).reshape(H, num_heads)[None, :, :, None, None]
        y = y + kv * skip
        out = jnp.einsum('bhijl,bhil->bhjl', y, x1r)
        return out.reshape(B, D, L)

    def _L0_ffn_ref(hidden_states, gate_w, expert_gate_up, expert_down, shared_gate_up, shared_down, shared_gate_vec):
        import jax, jax.numpy as jnp
        import numpy as np
        B, S, H = (4, 128, 256)
        E, K, I, SI = (16, 4, 176, 704)

        def _silu_mul(gu, inter):
            return jax.nn.silu(gu[:, :inter]) * gu[:, inter:]
        orig_shape = hidden_states.shape
        x = hidden_states.reshape(-1, H)
        router_logits = x @ gate_w.T
        routing_probs = jax.nn.softmax(router_logits.astype(jnp.float32), axis=-1)
        topk_w, topk_idx = jax.lax.top_k(routing_probs, K)
        topk_w = topk_w / topk_w.sum(axis=-1, keepdims=True)
        topk_w = topk_w.astype(x.dtype)
        combine = (jax.nn.one_hot(topk_idx, E, dtype=x.dtype) * topk_w[..., None]).sum(1)
        shared = _silu_mul(x @ shared_gate_up.T, SI) @ shared_down.T
        shared = shared * jax.nn.sigmoid(x @ shared_gate_vec.T)

        def step(acc, ew):
            w_gu, w_d, cw = ew
            h = _silu_mul(x @ w_gu.T, I)
            return (acc + h @ w_d.T * cw[:, None], None)
        acc0 = jnp.zeros_like(x)
        sparse, _ = jax.lax.scan(step, acc0, (expert_gate_up, expert_down, combine.T))
        return (shared + sparse).reshape(orig_shape)
    x = x + _L0_attn_ref(_layernorm(x, axis=-1), L0_attn_W_Q, L0_attn_b_Q, L0_attn_W_K, L0_attn_b_K, L0_attn_W_V, L0_attn_b_V, L0_attn_W_O, L0_attn_b_O)
    x = x + _L0_xattn_ref(_layernorm(x, axis=-1), L0_xattn_k, fside_S2_0, ctx_2048, ctx_2048, 8)
    x = x + _L0_ffn_ref(_layernorm(x, axis=-1), L0_ffn_gate_w, L0_ffn_expert_gate_up, L0_ffn_expert_down, L0_ffn_shared_gate_up, L0_ffn_shared_down, L0_ffn_shared_gate_vec)
    return x

_drawn_inputs = setup_inputs


def setup_inputs(seed=0):
    import zlib

    import numpy as np

    out = dict(_drawn_inputs(seed))
    spreads = {'L0_attn_b_Q': (0.0, 0.8),
     'L0_attn_b_K': (0.0, 0.8),
     'L0_attn_b_V': (0.0, 0.1),
     'L0_attn_b_O': (0.0, 0.1)}
    factors = {'L0_attn_W_Q': 8.0,
     'L0_attn_W_K': 8.0,
     'L0_ffn_gate_w': 8.0,
     'L0_ffn_expert_gate_up': 8.0,
     'L0_ffn_expert_down': 8.0,
     'L0_ffn_shared_gate_up': 8.0,
     'L0_ffn_shared_down': 8.0,
     'L0_ffn_shared_gate_vec': 8.0}
    for name, (base, spread) in spreads.items():
        noise = np.random.default_rng([zlib.crc32(name.encode()), seed]).standard_normal(out[name].shape)
        drawn = base * np.exp(spread * noise) if base else spread * noise
        out[name] = jnp.asarray(drawn.astype(out[name].dtype))
    for name, factor in factors.items():
        out[name] = (out[name] * factor).astype(out[name].dtype)
    return out
```

```python
import numpy as np
import concourse.bass as bass
from concourse import mybir
from contextlib import ExitStack

F32 = mybir.dt.float32
F32R = mybir.dt.float32r
ALU = mybir.AluOpType
ACT = mybir.ActivationFunctionType
AX = mybir.AxisListType

BATCH, SEQ, D = 16, 128, 256
HEADS, DH = 16, 128
PAIRS = HEADS // 2
GB = 4
GROUPS = BATCH // GB
GT = GB * SEQ
CH = D // 128
PW = 6 * 128
QE, QO, KE, KO, VV = 0, 128, 256, 384, 512
EPS = 1e-5
SCALE = float(DH) ** -0.5
MASKED = -1e30

RANKS = 8
FILTERS = SEQ // RANKS
HB = BATCH // 2

EXPERTS, TOPK, INTER, SHARED = 16, 4, 176, 704
UNITS = EXPERTS + SHARED // INTER
FEATS = UNITS * INTER
FCH = (FEATS + 127) // 128
FGRP = (FCH + 3) // 4
LOW_BYTES = 79 * 1024
LG = EXPERTS + 1


def decoder(nc, x_in, wqkv_in, bqk_in, bv_in, wo_in, bo_in, cos_in, sin_in, mask_in, ident_in,
            ctx_in, skip_in, kpad_in, same_in, turned_in, gate_in, gu_in, down_in, iota_in, out):
    with ExitStack() as ctx:
        def sb(name, shape, dt=F32, c=ctx):
            return c.enter_context(nc.sbuf_tensor(name, shape, dt))

        def bank(name):
            return ctx.enter_context(nc.psum_tensor(name, [128, 512], F32))

        def sem(name):
            return ctx.enter_context(nc.semaphore(name))

        banks = [bank(f"bank{i}") for i in range(8)]

        x = sb("x", [128, BATCH + 1, D])
        ident = sb("ident", [128, 128])
        stats = sb("stats", [128, BATCH, 6])
        mv = sb("mv", [128, BATCH + 1, 2])
        rstd = sb("rstd", [128, BATCH + 1])
        var = sb("var", [128, BATCH])
        newton = sb("newton", [128, BATCH])

        actx = ExitStack()
        xhat = sb("xhat", [128, GB, D], c=actx)
        xt_hi = sb("xt_hi", [128, CH, GT], F32R, actx)
        xt_lo = sb("xt_lo", [128, CH, GT], F32R, actx)
        raw = [sb(f"raw{i}", [128, PW], c=actx) for i in range(2)]
        w_hi = sb("w_hi", [128, PAIRS, CH, PW], F32R, actx)
        w_lo = sb("w_lo", [128, PAIRS, CH, PW], F32R, actx)
        wo = sb("wo", [128, HEADS, D], c=actx)
        bqk = sb("bqk", [128, PAIRS, 4], c=actx)
        bv = sb("bv", [128, HEADS], c=actx)
        bo = sb("bo", [128, D], c=actx)
        const = sb("const", [128, D], c=actx)
        cos = sb("cos", [128, SEQ], c=actx)
        sin = sb("sin", [128, SEQ], c=actx)
        mask = sb("mask", [128, SEQ], c=actx)
        turn = [[sb(f"turn{m}{i}", [128, GT], c=actx) for i in range(4)] for m in range(2)]
        rot = [[sb(f"rot{m}{h}", [128, GT], c=actx) for h in range(2)] for m in range(2)]
        v = [sb(f"v{i}", [128, GB, 2 * DH], c=actx) for i in range(2)]
        prob = [sb(f"prob{h}", [128, GB, SEQ], c=actx) for h in range(2)]
        prob_t = [sb(f"prob_t{h}", [128, GB, SEQ], c=actx) for h in range(2)]
        z_t = [sb(f"z_t{h}", [128, GB, SEQ], c=actx) for h in range(2)]
        negmax = sb("negmax", [128, 2, GB], c=actx)
        total = sb("total", [128, 2, GB], c=actx)
        rtotal = sb("rtotal", [128, 2, GB], c=actx)
        bv_wide = [*prob_t, *z_t]
        proj = banks[0:2]
        score = banks[2:4]
        pt_bank, zt_bank = banks[4], banks[5]
        acc = banks[6:8]

        actx.close()

        bctx = ExitStack()
        ctxg = [sb(f"ctxg{i}", [128, GB, D], c=bctx) for i in range(2)]
        xn = sb("xn", [128, GB, D], c=bctx)
        vcs = sb("vcs", [128, GB, D], c=bctx)
        dc = vcs
        v_t = sb("v_t", [128, CH, BATCH, SEQ], c=bctx)
        c_t = sb("c_t", [128, CH, BATCH, SEQ], c=bctx)
        o_t = sb("o_t", [128, CH, BATCH, SEQ], c=bctx)
        toep = [sb(f"toep{i}", [128, D], c=bctx) for i in range(2)]
        kv = [[sb(f"kv{i}{c}", [128, HB, RANKS, RANKS], c=bctx) for c in range(CH)] for i in range(2)]
        zc = [sb(f"zc{c}", [128, HB, RANKS, RANKS], c=bctx) for c in range(CH)]
        skip = sb("skip", [128, 1], c=bctx)
        same = sb("same", [128, 128], c=bctx)
        turned = sb("turned", [128, 128], c=bctx)
        bctx.close()
        cctx = ExitStack()
        gu_hi = sb("gu_hi", [128, UNITS, CH, 2 * INTER], F32R, c=cctx)
        xg = sb("xg", [128, GB, D], c=cctx)
        xgt = sb("xgt", [128, CH, GT], c=cctx)
        logit = sb("logit", [128, BATCH, LG], c=cctx)
        top = sb("top", [128, BATCH, 8], c=cctx)
        topi = sb("topi", [128, BATCH, 8], mybir.dt.uint32, cctx)
        topf = sb("topf", [128, BATCH, 8], c=cctx)
        hit = sb("hit", [128, 2, BATCH, EXPERTS], c=cctx)
        chosen = sb("chosen", [128, BATCH, EXPERTS], c=cctx)
        expl = sb("expl", [128, BATCH, LG], c=cctx)
        wsum = sb("wsum", [128, BATCH], c=cctx)
        weight = sb("weight", [128, BATCH, LG], c=cctx)
        silu = [sb(f"silu{i}", [128, INTER], c=cctx) for i in range(4)]
        cctx.close()
        ectx = ExitStack()
        sb("below", [128, LOW_BYTES // 4], c=ectx)
        dctx = ExitStack()
        gu_raw = sb("gu_raw", [128, UNITS, CH, 2 * INTER], c=dctx)
        dctx.close()
        gu_lo = sb("gu_lo", [128, UNITS, CH, 2 * INTER], F32R, ectx)
        down = sb("down", [128, FCH, D], c=ectx)
        gate = sb("gate", [128, CH, LG], c=ectx)
        iota = sb("iota", [128, EXPERTS], c=ectx)
        dctx = ExitStack()
        toep_all = sb("toep_all", [128, FILTERS, D], c=dctx)
        dctx.close()
        h_sb = sb("h_sb", [128, FEATS], c=ectx)
        h_t = [sb(f"h_t{i}", [128, 4, 128], c=ectx) for i in range(2)]
        xe = [sb(f"xe{i}", [128, D], c=ectx) for i in range(2)]
        xe_hi = [sb(f"xe_hi{i}", [128, CH, 128], F32R, ectx) for i in range(2)]
        xe_lo = [sb(f"xe_lo{i}", [128, CH, 128], F32R, ectx) for i in range(2)]
        ectx.close()

        x_in_sem = [sem(f"x_loaded{g}") for g in range(GROUPS)]
        small_loaded = sem("small_loaded")
        wo_loaded = sem("wo_loaded")
        raw_loaded = [sem(f"raw_loaded{i}") for i in range(2)]
        w_hi_done = sem("w_hi_done")
        w_lo_done = sem("w_lo_done")
        spare_set = sem("spare_set")
        stats_done = sem("stats_done")
        var_ready = sem("var_ready")
        rstd_ready = sem("rstd_ready")
        newton_done = sem("newton_done")
        xhat_ready = sem("xhat_ready")
        xt_ready = sem("xt_ready")
        xt_hi_done = sem("xt_hi_done")
        xt_lo_done = sem("xt_lo_done")
        qk_ready = sem("qk_ready")
        qk_used = sem("qk_used")
        rot_dve = sem("rot_dve")
        rot_pool = sem("rot_pool")
        v_ready = sem("v_ready")
        v_taken = sem("v_taken")
        s_ready = sem("s_ready")
        s_taken = sem("s_taken")
        max_ready = sem("max_ready")
        exp_done = sem("exp_done")
        rtotal_ready = sem("rtotal_ready")
        prob_ready = sem("prob_ready")
        pt_ready = sem("pt_ready")
        pt_taken = sem("pt_taken")
        zt_ready = sem("zt_ready")
        zt_taken = sem("zt_taken")
        wo_done = sem("wo_done")
        acc_taken = sem("acc_taken")
        bv_spread = sem("bv_spread")
        const_summed = sem("const_summed")
        const_ready = sem("const_ready")
        const_added = sem("const_added")
        ctx_loaded = [sem(f"ctx_loaded{i}") for i in range(2)]
        conv_loaded = sem("conv_loaded")
        gu_loaded = sem("gu_loaded")
        down_loaded = sem("down_loaded")
        xn_ready = sem("xn_ready")
        vcs_ready = sem("vcs_ready")
        vt_ready = sem("vt_ready")
        vt_taken = sem("vt_taken")
        ct_ready = sem("ct_ready")
        ct_taken = sem("ct_taken")
        skip_summed = sem("skip_summed")
        skip_taken = sem("skip_taken")
        skip_added = sem("skip_added")
        toep_turned = sem("toep_turned")
        toep_taken = sem("toep_taken")
        toep_ready = sem("toep_ready")
        kv_ready = sem("kv_ready")
        y_ready = sem("y_ready")
        y_taken = sem("y_taken")
        o_ready = sem("o_ready")
        back_ready = sem("back_ready")
        back_added = sem("back_added")
        gu_hi_done = sem("gu_hi_done")
        gu_lo_done = sem("gu_lo_done")
        xg_ready = sem("xg_ready")
        xgt_ready = sem("xgt_ready")
        xgt_taken = sem("xgt_taken")
        logit_ready = sem("logit_ready")
        route = sem("route")
        top_done = sem("top_done")
        exp_ready = sem("exp_ready")
        weight_ready = sem("weight_ready")
        xe_ready = sem("xe_ready")
        xet_ready = sem("xet_ready")
        xe_hi_done = sem("xe_hi_done")
        xe_lo_done = sem("xe_lo_done")
        up_ready = sem("up_ready")
        silu_ready = sem("silu_ready")
        h_ready = sem("h_ready")
        ht_ready = sem("ht_ready")
        ht_taken = sem("ht_taken")
        down_used = sem("down_used")
        y_added = sem("y_added")
        stored = sem("stored")

        block = ctx.enter_context(nc.Block())

        def attention(step, eng):
            for p in range(PAIRS):
                step(0, p, lambda k, p=p: p >= k, True)
            with eng.Fori(1, GROUPS) as g:
                for p in range(PAIRS):
                    step(g, p, lambda k: True, False)
            for p in range(3):
                step(GROUPS, p, lambda k, p=p: p < k, False)

        @block.sync
        def _(sp):
            sp.dma_start(x[:, 0:GB, :], x_in[:, 0:GB, :]).then_inc(x_in_sem[0], 16)
            sp.dma_start(ident[:], ident_in).then_inc(small_loaded, 16)
            n = 0
            for p in range(PAIRS):
                for c in range(CH):
                    if n >= 2:
                        sp.wait_ge(w_hi_done, n - 1)
                        sp.wait_ge(w_lo_done, n - 1)
                    sp.dma_start(raw[n % 2][:], wqkv_in[p, c]).then_inc(raw_loaded[n % 2], 16)
                    n += 1
                if p == 0:
                    sp.dma_start(bqk[:], bqk_in).then_inc(small_loaded, 16)
                    sp.dma_start(cos[:], cos_in).then_inc(small_loaded, 16)
                    sp.dma_start(sin[:], sin_in).then_inc(small_loaded, 16)
                    sp.dma_start(mask[:], mask_in).then_inc(small_loaded, 16)
                    sp.dma_start(bv[:], bv_in).then_inc(small_loaded, 16)
                    sp.dma_start(bo[:], bo_in.partition_broadcast(128)).then_inc(small_loaded, 16)
                    for g in range(1, GROUPS):
                        sp.dma_start(x[:, g * GB:(g + 1) * GB, :],
                                     x_in[:, g * GB:(g + 1) * GB, :]).then_inc(x_in_sem[g], 16)
                if p == 0:
                    sp.dma_start(wo[:], wo_in).then_inc(wo_loaded, 16)
            sp.wait_ge(acc_taken, 2 * GROUPS)
            sp.dma_start(skip[:], skip_in).then_inc(conv_loaded, 16)
            sp.dma_start(same[:], same_in).then_inc(conv_loaded, 16)
            sp.dma_start(turned[:], turned_in).then_inc(conv_loaded, 16)
            for g in range(2):
                sp.dma_start(ctxg[g][:], ctx_in[:, g * GB:(g + 1) * GB, :]).then_inc(ctx_loaded[g], 16)
            for f in range(FILTERS):
                line = kpad_in[f]
                sp.dma_start(toep_all[:, f, :],
                             bass.AP(tensor=line.tensor, offset=line.offset + 1, ap=[[1, 128], [1, D]])).then_inc(conv_loaded, 16)
            for g in range(2, GROUPS):
                sp.wait_ge(skip_taken, 2 * g - 2)
                sp.dma_start(ctxg[g % 2][:], ctx_in[:, g * GB:(g + 1) * GB, :]).then_inc(ctx_loaded[g % 2], 16)
            sp.dma_start(gate[:], gate_in).then_inc(gu_loaded, 16)
            sp.dma_start(iota[:], iota_in).then_inc(gu_loaded, 16)
            for part in range(4):
                u = slice(part * UNITS // 4, (part + 1) * UNITS // 4)
                sp.dma_start(gu_raw[:, u], gu_in[:, u]).then_inc(gu_loaded, 16)
            sp.dma_start(down[:, 0:FCH - 1, :], down_in[0:(FCH - 1) * 128].rearrange("(c p) n -> p c n", p=128)).then_inc(down_loaded, 16)
            sp.dma_start(down[0:FEATS - (FCH - 1) * 128, FCH - 1, :], down_in[(FCH - 1) * 128:FEATS]).then_inc(down_loaded, 16)
            with sp.Fori(0, BATCH) as b:
                sp.wait_ge(y_added, b + 1)
                sp.dma_start(out[:, bass.ds(b, 1), :], x[:, bass.ds(b, 1), :]).then_inc(stored, 16)
            sp.wait_ge(stored, 16 * BATCH)

        CONV = (3 + FILTERS) * 16
        GU = 6 * 16

        def halves(step, eng):
            step(0, 0, True)
            step(1, 1, True)
            with eng.Fori(1, FILTERS // 2) as n:
                step(n * 2, 0, False)
                step(n * 2 + 1, 1, False)

        def experts(step, eng):
            step(0, 0, lambda k: k == 0)
            step(1, 1, lambda k: True)
            with eng.Fori(1, BATCH // 2) as n:
                step(n * 2, 0, lambda k: True)
                step(n * 2 + 1, 1, lambda k: True)
            step(BATCH, 0, lambda k: k == 1)

        SMALL = 7 * 16

        @block.tensor
        def _(pe):
            pe.wait_ge(small_loaded, SMALL)

            def product3(o, parts):
                n = len(parts)
                for i, (lh, ll, rh, rl) in enumerate(parts):
                    nc.tensor.matmul(o, lh, rh, start=(i == 0), stop=False)
                    nc.tensor.matmul(o, lh, rl, start=False, stop=False)
                    last = nc.tensor.matmul(o, ll, rh, start=False, stop=(i == n - 1))
                return last

            def project(p, col, o):
                return product3(o, [(w_hi[:, p, c, col:col + 128], w_lo[:, p, c, col:col + 128],
                                     xt_hi[:, c, :], xt_lo[:, c, :]) for c in range(CH)])

            def transpose_probs(s, p, h, first):
                pe.wait_ge(prob_ready, s * 2 - 4 + h + 1)
                if not (first and p == 2 and h == 0):
                    pe.wait_ge(pt_taken, s * 2 - 4 + h)
                for b in range(GB):
                    last = nc.tensor.transpose(pt_bank[:, b * 128:(b + 1) * 128],
                                               prob[h][:, b, :], ident[:])
                last.then_inc(pt_ready, 1)

            def weigh_values(s, p, h, first):
                pe.wait_ge(pt_taken, s * 2 - 4 + h + 1)
                if not (first and p == 2 and h == 0):
                    pe.wait_ge(zt_taken, s * 2 - 4 + h)
                for b in range(GB):
                    last = nc.tensor.matmul(zt_bank[:, b * 128:(b + 1) * 128],
                                            v[p % 2][:, b, h * DH:(h + 1) * DH],
                                            prob_t[h][:, b, :], start=True, stop=True)
                last.then_inc(zt_ready, 1)

            def step(g, p, live, first):
                s = g * PAIRS + p
                if live(1):
                    q = (p - 1) % PAIRS
                    for half in range(2):
                        pe.wait_ge(qk_used, s * 4 - 1 + half)
                        for b in range(2):
                            t = (2 * half + b) * SEQ
                            last = product3(proj[half][:, b * 256:(b + 1) * 256],
                                            [(xt_hi[:, c, t:t + SEQ], xt_lo[:, c, t:t + SEQ],
                                              w_hi[:, q, c, VV:VV + 256], w_lo[:, q, c, VV:VV + 256])
                                             for c in range(CH)])
                        last.then_inc(v_ready, 1)
                if p == 0 and live(0):
                    pe.wait_ge(xhat_ready, g * GB + GB)
                    for c in range(CH):
                        if not first:
                            pe.wait_ge(v_taken, s * 2 - 1 + c)
                        for b in range(GB):
                            last = nc.tensor.transpose(proj[c][:, b * 128:(b + 1) * 128],
                                                       xhat[:, b, c * 128:(c + 1) * 128], ident[:])
                        last.then_inc(xt_ready, 1)
                if live(2):
                    transpose_probs(s, p, 0, first)
                if live(3):
                    r = (p - 3) % PAIRS
                    pe.wait_ge(zt_taken, s * 2 - 4)
                    if r == 0:
                        if first:
                            pe.wait_ge(const_ready, 1)
                        else:
                            pe.wait_ge(acc_taken, g * 2)
                    for b in range(GB):
                        for h in range(2):
                            last = nc.tensor.matmul(
                                acc[b // 2][:, (b % 2) * D:(b % 2 + 1) * D], z_t[h][:, b, :],
                                wo[:, 2 * r + h, :], start=(r == 0 and b % 2 == 0 and h == 0),
                                stop=(r == PAIRS - 1 and h == 1), skip_group_check=True)
                    last.then_inc(wo_done, 1)
                if live(2):
                    weigh_values(s, p, 0, first)
                    transpose_probs(s, p, 1, first)
                if live(1):
                    pe.wait_ge(rot_dve, s * 4)
                    pe.wait_ge(rot_pool, s * 4)
                    for h in range(2):
                        if live(2):
                            pe.wait_ge(s_taken, s * 2 - 4 + h + 1)
                        for b in range(GB):
                            t = slice(b * SEQ, (b + 1) * SEQ)
                            last = nc.tensor.matmul(score[h][:, t], rot[0][h][:, t], rot[1][h][:, t],
                                                    start=True, stop=True)
                        last.then_inc(s_ready, 1)
                for i, col in enumerate((QE, QO, KE, KO)):
                    if live(0):
                        if first and i == 0:
                            pe.wait_ge(w_hi_done, 2 * p + 2)
                            pe.wait_ge(w_lo_done, 2 * p + 2)
                        if i < 2 and p == 0:
                            pe.wait_ge(xt_hi_done, g * 2 + 2)
                            pe.wait_ge(xt_lo_done, g * 2 + 2)
                        elif i < 2:
                            pe.wait_ge(v_taken, s * 2 - 1 + i)
                        else:
                            pe.wait_ge(qk_used, s * 4 + i - 1)
                        project(p, col, proj[i % 2][:]).then_inc(qk_ready, 1)
                    if i == 0 and live(2):
                        weigh_values(s, p, 1, first)
                if first and p == 1:
                    pe.wait_ge(wo_loaded, 16)
                    pe.wait_ge(bv_spread, 4)
                    for n in range(HEADS):
                        last = nc.tensor.matmul(acc[0][:, 0:D], bv_wide[n // 4][:, n % 4, :], wo[:, n, :],
                                                start=(n == 0), stop=(n == HEADS - 1))
                    last.then_inc(const_summed, 1)

            attention(step, pe)

            pe.wait_ge(conv_loaded, CONV)
            with pe.Fori(0, FILTERS // 4) as n:
                for i in range(2):
                    nc.tensor.matmul(banks[6 + i][:], turned[:], toep_all[:, bass.ds(n * 4 + 2 * i, 2), :],
                                     start=True, stop=True).then_inc(toep_turned, 1)
                pe.wait_ge(toep_taken, n * 2 + 2)
            with pe.Fori(0, GROUPS // 2) as n:
                for i in range(2):
                    g = n * 2 + i
                    pe.wait_ge(xn_ready, g * GB + GB)
                    for c in range(CH):
                        for b in range(GB):
                            last = nc.tensor.transpose(banks[c][:, b * 128:(b + 1) * 128],
                                                       xn[:, b, c * 128:(c + 1) * 128], ident[:])
                        last.then_inc(vt_ready, 1)
                    pe.wait_ge(ctx_loaded[i], n * 16 + 16)
                    for c in range(CH):
                        for b in range(GB):
                            last = nc.tensor.transpose(banks[2 + c][:, b * 128:(b + 1) * 128],
                                                       ctxg[i][:, b, c * 128:(c + 1) * 128], ident[:])
                        last.then_inc(ct_ready, 1)
                    pe.wait_ge(vcs_ready, g + 1)
                    for j in range(2):
                        nc.tensor.matmul(banks[4 + j][:], same[:], vcs[:, 2 * j:2 * j + 2, :], start=True,
                                         stop=True).then_inc(skip_summed, 1)
                    pe.wait_ge(vt_taken, g * 2 + 2)
                    pe.wait_ge(ct_taken, g * 2 + 2)
                    pe.wait_ge(skip_taken, g * 2 + 2)

            def conv_step(f, i, first):
                pe.wait_ge(toep_ready, f + 1)
                for half in range(2):
                    u = f * 2 + half
                    if not (first and i == 0):
                        pe.wait_ge(y_taken, u * 2 - 2)
                    pe.wait_ge(kv_ready, u * 2 + 1)
                    nc.tensor.matmul(banks[2 * half][:], toep[i][:, 0:128], kv[half][0][:],
                                     start=True, stop=True).then_inc(y_ready, 1)
                    pe.wait_ge(kv_ready, u * 2 + 2)
                    nc.tensor.matmul(banks[2 * half + 1][:], toep[i][:, 128:256], kv[half][0][:], start=True, stop=False)
                    nc.tensor.matmul(banks[2 * half + 1][:], toep[i][:, 0:128], kv[half][1][:],
                                     start=False, stop=True).then_inc(y_ready, 1)

            halves(conv_step, pe)

            pe.wait_ge(o_ready, 4 * FILTERS)
            pe.wait_ge(y_taken, 4 * FILTERS)
            for j in range(BATCH // 2):
                if j >= 4:
                    pe.wait_ge(back_added, j - 3)
                for b in range(2):
                    for c in range(CH):
                        last = nc.tensor.transpose(banks[4 + j % 4][:, (2 * b + c) * 128:(2 * b + c + 1) * 128],
                                                   o_t[:, c, 2 * j + b, :], ident[:])
                last.then_inc(back_ready, 1)

            pe.wait_ge(gu_loaded, GU)
            pe.wait_ge(back_added, BATCH // 2)
            with pe.Fori(0, GROUPS) as g:
                pe.wait_ge(xg_ready, g * GB + GB)
                for c in range(CH):
                    for b in range(GB):
                        last = nc.tensor.transpose(banks[c][:, b * 128:(b + 1) * 128],
                                                   xg[:, b, c * 128:(c + 1) * 128], ident[:])
                    last.then_inc(xgt_ready, 1)
                pe.wait_ge(xgt_taken, g * 2 + 2)
                for b in range(GB):
                    for c in range(CH):
                        last = nc.tensor.matmul(banks[2][:, bass.ds(g * (GB * LG) + b * LG, LG)],
                                                xgt[:, c, b * 128:(b + 1) * 128], gate[:, c, :],
                                                start=(c == 0), stop=(c == CH - 1), skip_group_check=True)
                last.then_inc(logit_ready, 1)

            def unit_up(b, q, e, first):
                if first:
                    pe.wait_ge(gu_hi_done, e + 1)
                    pe.wait_ge(gu_lo_done, e + 1)
                if not (first and e < 4):
                    pe.wait_ge(h_ready, b * UNITS + e - 3)
                product3(banks[e % 4][:, 0:2 * INTER],
                         [(xe_hi[q][:, c, :], xe_lo[q][:, c, :], gu_hi[:, e, c, :], gu_lo[:, e, c, :])
                          for c in range(CH)]).then_inc(up_ready, 1)

            def h_transposed(b, q, k, first):
                pe.wait_ge(h_ready, b * UNITS + min(UNITS, (512 * (k + 1) + INTER - 1) // INTER))
                n = b * FGRP + k
                if not (first and k < 2):
                    pe.wait_ge(ht_taken, n - 1)
                bank = banks[4 + (q * FGRP + k) % 2]
                for j in range(min(4, FCH - 4 * k)):
                    f = 128 * (4 * k + j)
                    w = min(128, FEATS - f)
                    last = nc.tensor.transpose(bank[0:w, j * 128:(j + 1) * 128], h_sb[:, f:f + w], ident[:])
                last.then_inc(ht_ready, 1)

            def h_down(b, q, k):
                pe.wait_ge(ht_taken, b * FGRP + k + 1)
                for j in range(min(4, FCH - 4 * k)):
                    c = 4 * k + j
                    w = min(128, FEATS - 128 * c)
                    last = nc.tensor.matmul(banks[6][:, 0:D], h_t[(q * FGRP + k) % 2][0:w, j, :], down[0:w, c, :],
                                            start=(c == 0), stop=(c == FCH - 1))
                last.then_inc(down_used, 1)

            T_AT = [4, 7, 10, 13, 16, 19, 22]
            D_AT = [6, 9, 12, 15, 18, 21, 24]

            def expert_step(b, q, live):
                first = not live(1)
                if live(0):
                    if first:
                        pe.wait_ge(route, 1)
                    pe.wait_ge(xe_ready, b + 1)
                    if not first:
                        pe.wait_ge(xe_lo_done, b * 2)
                    for c in range(CH):
                        last = nc.tensor.transpose(banks[7][:, c * 128:(c + 1) * 128],
                                                   xe[q][:, c * 128:(c + 1) * 128], ident[:])
                    last.then_inc(xet_ready, 1)
                    pe.wait_ge(xe_hi_done, b + 1)
                    pe.wait_ge(xe_lo_done, b * 2 + 2)
                for e in range(UNITS):
                    if live(0):
                        unit_up(b, q, e, first)
                    for k in range(FGRP):
                        if T_AT[k] == e and live(0):
                            h_transposed(b, q, k, first)
                        if T_AT[k] == e + UNITS and live(1):
                            h_transposed(b - 1, 1 - q, k, False)
                        if D_AT[k] == e and live(0):
                            if k == 0 and not first:
                                pe.wait_ge(y_added, b)
                            h_down(b, q, k)
                        if D_AT[k] == e + UNITS and live(1):
                            h_down(b - 1, 1 - q, k)

            pe.wait_ge(down_loaded, 32)
            experts(expert_step, pe)

        @block.scalar
        def _(act):
            def split_hi(n):
                act.wait_ge(raw_loaded[n % 2], 16 * (n // 2 + 1))
                nc.scalar.copy(w_hi[:, n // CH, n % CH, :], raw[n % 2][:]).then_inc(w_hi_done, 1)

            def root(k):
                act.wait_ge(var_ready, 2 * k + 2)
                nc.scalar.activation(rstd[:, 0:BATCH], newton[:], ACT.Sqrt).then_inc(rstd_ready, 1)

            root(0)
            split_hi(0)
            split_hi(1)

            def step(g, p, live, first):
                s = g * PAIRS + p

                def exps(h):
                    act.wait_ge(max_ready, s * 2 - 2 + h + 1)
                    for b in range(GB):
                        last = nc.scalar.activation(prob[h][:, b, :], prob[h][:, b, :], ACT.Exp,
                                                    bias=negmax[:, h, b:b + 1],
                                                    accum_out=total[:, h, b:b + 1])
                    last.then_inc(exp_done, 1)

                if live(1):
                    for half in range(2):
                        act.wait_ge(v_ready, s * 2 - 2 + half + 1)
                        if live(3):
                            act.wait_ge(zt_ready, s * 2 - 4)
                        nc.scalar.copy(v[(p - 1) % 2][:, 2 * half:2 * half + 2, :],
                                       proj[half][:].rearrange("p (b n) -> p b n", b=2)).then_inc(v_taken, 1)
                if p == 0 and live(0):
                    for c in range(CH):
                        act.wait_ge(xt_ready, g * 2 + c + 1)
                        nc.scalar.copy(xt_hi[:, c, :], proj[c][:]).then_inc(xt_hi_done, 1)
                if first and p < PAIRS - 1:
                    split_hi(2 * p + 2)
                    split_hi(2 * p + 3)
                if live(2):
                    for i in range(4):
                        h = i // 2
                        if i in (0, 2):
                            act.wait_ge(pt_ready, s * 2 - 4 + h + 1)
                            if live(3):
                                act.wait_ge(zt_ready, s * 2 - 6 + h + 1)
                            nc.scalar.copy(prob_t[h][:], pt_bank[:].rearrange("p (b n) -> p b n", b=GB)).then_inc(pt_taken, 1)
                        else:
                            act.wait_ge(zt_ready, s * 2 - 4 + h + 1)
                            if live(3):
                                act.wait_ge(wo_done, s - 2)
                            nc.scalar.copy(z_t[h][:], zt_bank[:].rearrange("p (b n) -> p b n", b=GB)).then_inc(zt_taken, 1)
                if live(1):
                    exps(0)
                    exps(1)

            attention(step, act)

            with act.Fori(0, FILTERS // 4) as n:
                for i in range(2):
                    act.wait_ge(toep_turned, n * 2 + i + 1)
                    nc.scalar.copy(toep_all[:, bass.ds(n * 4 + 2 * i, 2), :],
                                   banks[6 + i][:].rearrange("p (f l) -> p f l", f=2)).then_inc(toep_taken, 1)
            root(1)
            with act.Fori(0, GROUPS) as g:
                for c in range(CH):
                    act.wait_ge(vt_ready, g * 2 + c + 1)
                    nc.scalar.copy(v_t[:, c, bass.ds(g * GB, GB), :],
                                   banks[c][:].rearrange("p (b t) -> p b t", b=GB)).then_inc(vt_taken, 1)

            act.wait_ge(toep_taken, FILTERS // 2)

            def toep_step(f, i, first):
                if not first:
                    act.wait_ge(y_ready, f * 4 - 4)
                src = toep_all[:, i, :] if first else toep_all[:, bass.ds(f, 1), :].rearrange("p a n -> p (a n)")
                nc.scalar.copy(toep[i][:], src).then_inc(toep_ready, 1)

            halves(toep_step, act)

            root(2)
            with act.Fori(0, GROUPS) as g:
                for c in range(CH):
                    act.wait_ge(xgt_ready, g * 2 + c + 1)
                    nc.scalar.copy(xgt[:, c, :], banks[c][:]).then_inc(xgt_taken, 1)
                act.wait_ge(logit_ready, g + 1)
            act.wait_ge(route, 2)
            nc.scalar.activation(expl[:], expl[:], ACT.Exp).then_inc(exp_ready, 1)

            def split_unit(e):
                act.wait_ge(o_ready, 4 * FILTERS)
                act.wait_ge(back_ready, BATCH // 2)
                nc.scalar.copy(gu_hi[:, e], gu_raw[:, e]).then_inc(gu_hi_done, 1)

            def x_high(b, q):
                act.wait_ge(xet_ready, b + 1)
                nc.scalar.copy(xe_hi[q][:], banks[7][:, 0:D].rearrange("p (c t) -> p c t", c=CH)).then_inc(xe_hi_done, 1)

            T_AT = [4, 7, 10, 13, 16, 19, 22]

            def expert_step(b, q, live):
                first = not live(1)
                if first:
                    for e in range(UNITS):
                        split_unit(e)
                if live(0):
                    x_high(b, q)
                for e in range(UNITS):
                    if live(0):
                        act.wait_ge(up_ready, b * UNITS + e + 1)
                        if not (first and e < 4):
                            act.wait_ge(h_ready, b * UNITS + e - 3)
                        nc.scalar.activation(silu[e % 4][:], banks[e % 4][:, 0:INTER], ACT.Silu).then_inc(silu_ready, 1)
                    for k in range(FGRP):
                        if T_AT[k] == e and live(0):
                            h_take(b, q, k, first)
                        if T_AT[k] == e + UNITS and live(1):
                            h_take(b - 1, 1 - q, k, False)

            def h_take(b, q, k, first):
                n = b * FGRP + k
                act.wait_ge(ht_ready, n + 1)
                if not (first and k < 2):
                    act.wait_ge(down_used, n - 1)
                i = (q * FGRP + k) % 2
                full = min(4, FEATS // 128 - 4 * k)
                src = banks[4 + i][:].rearrange("p (j t) -> p j t", j=4)
                if full == 4:
                    nc.scalar.copy(h_t[i][:], src).then_inc(ht_taken, 1)
                else:
                    w = FEATS % 128
                    nc.scalar.copy(h_t[i][:, 0:full, :], src[:, 0:full, :])
                    nc.scalar.copy(h_t[i][0:w, full, :], src[0:w, full, :]).then_inc(ht_taken, 1)

            experts(expert_step, act)

        @block.gpsimd
        def _(pool):
            nc.gpsimd.memset(x[:, BATCH, :], 0.0)
            nc.gpsimd.memset(mv[:, BATCH, :], 0.0)
            nc.gpsimd.memset(rstd[:, BATCH:BATCH + 1], 0.0).then_inc(spare_set, 1)
            pool.wait_ge(small_loaded, SMALL)
            for i in range(4):
                nc.gpsimd.tensor_copy(bv_wide[i][:],
                                      bv[:, 4 * i:4 * i + 4].unsqueeze(2).to_broadcast([128, 4, 128])).then_inc(bv_spread, 1)
            pool.wait_ge(bv_spread, 4)

            def step(g, p, live, first):
                s = g * PAIRS + p
                for m in range(2):
                    if live(0):
                        pool.wait_ge(qk_used, s * 4 + 2 * m + 2)
                        if live(1):
                            pool.wait_ge(s_ready, s * 2)
                        pool_rot(m, s)
                    if m == 0 and live(1):
                        for h in range(2):
                            pool.wait_ge(rtotal_ready, s * 2 - 2 + h + 1)
                            nc.gpsimd.tensor_tensor(prob[h][:], prob[h][:],
                                                    rtotal[:, h, :].unsqueeze(2).to_broadcast([128, GB, SEQ]),
                                                    ALU.mult).then_inc(prob_ready, 1)
                        pool.wait_ge(prob_ready, s * 2)
                if p == 5 and live(0):
                    pool.wait_ge(const_ready, 1)
                    pool.wait_ge(xhat_ready, g * GB + GB)
                    xg = x[:, 0:GB, :] if first else x[:, bass.ds(g * GB, GB), :]
                    nc.gpsimd.tensor_tensor(xg, xg, const[:].unsqueeze(1).to_broadcast([128, GB, D]),
                                            ALU.add).then_inc(const_added, 1)
                    pool.wait_ge(const_added, g + 1)

            def pool_rot(m, s):
                nc.gpsimd.tensor_tensor(rot[m][0][0:64, :], turn[m][0][0:64, :], turn[m][2][0:64, :],
                                        ALU.subtract).then_inc(rot_pool, 1)
                pool.wait_ge(rot_pool, s * 4 + 2 * m + 1)
                nc.gpsimd.tensor_tensor(rot[m][1][64:128, :], turn[m][1][64:128, :], turn[m][3][64:128, :],
                                        ALU.add).then_inc(rot_pool, 1)
                pool.wait_ge(rot_pool, s * 4 + 2 * m + 2)

            attention(step, pool)

            with pool.Fori(0, GROUPS) as g:
                for j in range(2):
                    pool.wait_ge(skip_taken, g * 2 + j + 1)
                    xs = x[:, bass.ds(g * GB + 2 * j, 2), :]
                    nc.gpsimd.tensor_tensor(xs, xs, dc[:, 2 * j:2 * j + 2, :], ALU.add).then_inc(skip_added, 1)
            pool.wait_ge(vt_taken, 2 * GROUPS)
            pool.wait_ge(ct_taken, 2 * GROUPS)

            def kv_step(f, i, first):
                for half in range(2):
                    u = f * 2 + half
                    if not (first and i == 0):
                        pool.wait_ge(y_ready, u * 2 - 2)
                    ch = slice(i * RANKS, (i + 1) * RANKS) if first else bass.ds(f * RANKS, RANKS)
                    bs = slice(half * HB, (half + 1) * HB)
                    for c in range(CH):
                        nc.gpsimd.tensor_tensor(
                            kv[half][c][:],
                            v_t[:, c, bs, ch].unsqueeze(3).to_broadcast([128, HB, RANKS, RANKS]),
                            c_t[:, c, bs, ch].unsqueeze(2).to_broadcast([128, HB, RANKS, RANKS]),
                            ALU.mult).then_inc(kv_ready, 1)

            halves(kv_step, pool)

        @block.vector
        def _(dve):
            def token_stats(k):
                for b in range(BATCH):
                    if k == 0:
                        dve.wait_ge(x_in_sem[b // GB], 16)
                    nc.vector.bn_stats(stats[:, b, :], x[:, b, :]).then_inc(stats_done, 1)
                done = k * (BATCH + 1)
                for b in range(BATCH):
                    dve.wait_ge(stats_done, done + b + 1)
                    last = nc.vector.bn_aggr(mv[:, b, :], stats[:, b, :])
                last.then_inc(stats_done, 1)
                dve.wait_ge(stats_done, done + BATCH + 1)
                nc.vector.tensor_scalar(var[:], mv[:, 0:BATCH, 1], EPS, None, ALU.add).then_inc(var_ready, 1)
                dve.wait_ge(var_ready, 2 * k + 1)
                nc.vector.reciprocal(newton[:], var[:]).then_inc(var_ready, 1)
                dve.wait_ge(rstd_ready, k + 1)
                nc.vector.tensor_tensor(newton[:], rstd[:, 0:BATCH], rstd[:, 0:BATCH], ALU.mult).then_inc(newton_done, 1)
                dve.wait_ge(newton_done, 4 * k + 1)
                nc.vector.tensor_tensor(newton[:], newton[:], var[:], ALU.mult).then_inc(newton_done, 1)
                dve.wait_ge(newton_done, 4 * k + 2)
                nc.vector.tensor_scalar(newton[:], newton[:], -0.5, 1.5, ALU.mult, ALU.add).then_inc(newton_done, 1)
                dve.wait_ge(newton_done, 4 * k + 3)
                nc.vector.tensor_tensor(rstd[:, 0:BATCH], rstd[:, 0:BATCH], newton[:], ALU.mult).then_inc(newton_done, 1)
                dve.wait_ge(newton_done, 4 * k + 4)

            def normalise(dst, b, done):
                nc.vector.tensor_scalar(dst, x[:, bass.ds(b, 1), :].rearrange("p a n -> p (a n)"),
                                        mv[:, bass.ds(b, 1), 0:1].rearrange("p a n -> p (a n)"),
                                        rstd[:, bass.ds(b, 1)], ALU.subtract, ALU.mult).then_inc(done, 1)

            token_stats(0)
            dve.wait_ge(small_loaded, SMALL)

            def split_lo(n):
                dve.wait_ge(w_hi_done, n + 1)
                nc.vector.tensor_tensor(w_lo[:, n // CH, n % CH, :], raw[n % 2][:],
                                        w_hi[:, n // CH, n % CH, :].bitcast(F32), ALU.subtract).then_inc(w_lo_done, 1)

            def step(g, p, live, first):
                s = g * PAIRS + p
                if p == 0 and live(0):
                    if not first:
                        dve.wait_ge(xt_ready, g * 2)
                    for b in range(GB):
                        at = b if first else g * GB + b
                        xb = x[:, b, :] if first else x[:, bass.ds(at, 1), :].rearrange("p a n -> p (a n)")
                        m = mv[:, b, 0:1] if first else mv[:, bass.ds(at, 1), 0:1].rearrange("p a n -> p (a n)")
                        r = rstd[:, b:b + 1] if first else rstd[:, bass.ds(at, 1)]
                        nc.vector.tensor_scalar(xhat[:, b, :], xb, m, r, ALU.subtract, ALU.mult).then_inc(xhat_ready, 1)
                    for c in range(CH):
                        dve.wait_ge(xt_hi_done, g * 2 + c + 1)
                        nc.vector.tensor_tensor(xt_lo[:, c, :], proj[c][:], xt_hi[:, c, :].bitcast(F32),
                                                ALU.subtract).then_inc(xt_lo_done, 1)
                    if first:
                        split_lo(0)
                        split_lo(1)
                if live(1):
                    for h in range(2):
                        dve.wait_ge(s_ready, s * 2 - 2 + h + 1)
                        nc.vector.scalar_tensor_tensor(
                            prob[h][:], score[h][:].rearrange("p (b t) -> p b t", b=GB), SCALE,
                            mask[:].unsqueeze(1).to_broadcast([128, GB, SEQ]), ALU.mult, ALU.add).then_inc(s_taken, 1)
                        dve.wait_ge(s_taken, s * 2 - 2 + h + 1)
                        nc.vector.tensor_reduce(negmax[:, h, :], prob[h][:], AX.X, ALU.max, negate=True).then_inc(max_ready, 1)
                if p == 2 and live(3):
                    for i in range(2):
                        dve.wait_ge(wo_done, g * PAIRS)
                        dve.wait_ge(const_added, g)
                        xs = x[:, bass.ds(g * GB - GB + 2 * i, 2), :]
                        nc.vector.tensor_tensor(xs, acc[i][:].rearrange("p (b n) -> p b n", b=2), xs,
                                                ALU.add).then_inc(acc_taken, 1)
                for m in range(2):
                    t = turn[m]
                    if live(0):
                        for i, (part, tc, ts) in enumerate(((0, 0, 1), (1, 3, 2))):
                            dve.wait_ge(qk_ready, s * 4 + 2 * m + i + 1)
                            if i == 0:
                                if live(1):
                                    dve.wait_ge(rot_pool, s * 4 - 2 + 2 * m)
                                    dve.wait_ge(rot_dve, s * 4 - 2 + 2 * m)
                            src = proj[i][:].rearrange("p (b t) -> p b t", b=GB)
                            for dst, tab in ((tc, cos), (ts, sin)):
                                last = nc.vector.scalar_tensor_tensor(
                                    t[dst][:].rearrange("p (b t) -> p b t", b=GB), src,
                                    bqk[:, p, 2 * m + part:2 * m + part + 1],
                                    tab[:].unsqueeze(1).to_broadcast([128, GB, SEQ]), ALU.add, ALU.mult)
                            last.then_inc(qk_used, 1)
                        dve.wait_ge(qk_used, s * 4 + 2 * m + 2)
                        if live(1):
                            dve.wait_ge(s_ready, s * 2)
                        nc.vector.tensor_tensor(rot[m][1][0:64, :], t[0][64:128, :], t[2][64:128, :],
                                                ALU.subtract).then_inc(rot_dve, 1)
                        nc.vector.tensor_tensor(rot[m][0][64:128, :], t[1][0:64, :], t[3][0:64, :],
                                                ALU.add).then_inc(rot_dve, 1)
                    if m == 0 and live(1):
                        for h in range(2):
                            dve.wait_ge(exp_done, s * 2 - 2 + h + 1)
                            nc.vector.reciprocal(rtotal[:, h, :], total[:, h, :]).then_inc(rtotal_ready, 1)
                if first and p < PAIRS - 1:
                    split_lo(2 * p + 2)
                    split_lo(2 * p + 3)
                if first and p == 1:
                    dve.wait_ge(const_summed, 1)
                    nc.vector.tensor_tensor(const[:], acc[0][:, 0:D], bo[:], ALU.add).then_inc(const_ready, 1)

            attention(step, dve)

            dve.wait_ge(acc_taken, 2 * GROUPS)
            token_stats(1)
            dve.wait_ge(conv_loaded, CONV)
            with dve.Fori(0, GROUPS // 2) as n:
                for i in range(2):
                    g = n * 2 + i
                    for b in range(GB):
                        normalise(xn[:, b, :], g * GB + b, xn_ready)
                    dve.wait_ge(xn_ready, g * GB + GB)
                    dve.wait_ge(ctx_loaded[i], n * 16 + 16)
                    nc.vector.scalar_tensor_tensor(vcs[:], xn[:], skip[:], ctxg[i][:], ALU.mult, ALU.mult).then_inc(vcs_ready, 1)
                    for c in range(CH):
                        dve.wait_ge(ct_ready, g * 2 + c + 1)
                        nc.vector.tensor_copy(c_t[:, c, bass.ds(g * GB, GB), :],
                                              banks[2 + c][:].rearrange("p (b t) -> p b t", b=GB)).then_inc(ct_taken, 1)
                    for j in range(2):
                        dve.wait_ge(skip_summed, g * 2 + 2)
                        nc.vector.tensor_tensor(dc[:, 2 * j:2 * j + 2, :],
                                                banks[4 + j][:].rearrange("p (b n) -> p b n", b=2),
                                                ctxg[i][:, 2 * j:2 * j + 2, :], ALU.mult).then_inc(skip_taken, 1)
                    dve.wait_ge(vt_ready, g * 2 + 2)
                    dve.wait_ge(skip_added, g * 2 + 2)

            def z_step(f, i, first):
                for half in range(2):
                    u = f * 2 + half
                    ch = slice(i * RANKS, (i + 1) * RANKS) if first else bass.ds(f * RANKS, RANKS)
                    bs = slice(half * HB, (half + 1) * HB)
                    for c in range(CH):
                        dve.wait_ge(y_ready, u * 2 + c + 1)
                        if not (first and i == 0 and half == 0):
                            dve.wait_ge(o_ready, u * 2 - 2 + c + 1)
                        nc.vector.tensor_tensor(
                            zc[c][:], banks[2 * half + c][:].rearrange("p (b i j) -> p b i j", b=HB, i=RANKS),
                            c_t[:, c, bs, ch].unsqueeze(3).to_broadcast([128, HB, RANKS, RANKS]),
                            ALU.mult).then_inc(y_taken, 1)
                    for c in range(CH):
                        dve.wait_ge(y_taken, u * 2 + c + 1)
                        nc.vector.tensor_reduce(o_t[:, c, bs, ch], zc[c][:].rearrange("p b i j -> p b j i"),
                                                AX.X, ALU.add).then_inc(o_ready, 1)

            halves(z_step, dve)
            dve.wait_ge(skip_added, 2 * GROUPS)
            for j in range(BATCH // 2):
                dve.wait_ge(back_ready, j + 1)
                xs = x[:, 2 * j:2 * j + 2, :]
                nc.vector.tensor_tensor(xs, banks[4 + j % 4][:].rearrange("p (b n) -> p b n", b=2), xs,
                                        ALU.add).then_inc(back_added, 1)

            dve.wait_ge(back_added, BATCH // 2)
            token_stats(2)
            with dve.Fori(0, GROUPS) as g:
                for b in range(GB):
                    normalise(xg[:, b, :], g * GB + b, xg_ready)
                dve.wait_ge(xgt_ready, g * 2 + 2)
            dve.wait_ge(logit_ready, GROUPS)
            dve.wait_ge(gu_loaded, GU)
            nc.vector.tensor_copy(logit[:], banks[2][:, 0:BATCH * LG].rearrange("p (b e) -> p b e", b=BATCH)).then_inc(route, 1)
            dve.wait_ge(route, 1)
            for b in range(BATCH):
                last = nc.vector.max(top[:, b, :], logit[:, b, 0:EXPERTS])
            last.then_inc(top_done, 1)
            dve.wait_ge(top_done, 1)
            nc.vector.tensor_tensor(expl[:, :, 0:EXPERTS], logit[:, :, 0:EXPERTS],
                                    top[:, :, 0:1].to_broadcast([128, BATCH, EXPERTS]), ALU.subtract)
            nc.vector.tensor_scalar(expl[:, :, EXPERTS], logit[:, :, EXPERTS], -1.0, None, ALU.mult).then_inc(route, 1)
            for b in range(BATCH):
                last = nc.vector.max_index(topi[:, b, :], top[:, b, :], logit[:, b, 0:EXPERTS])
            last.then_inc(top_done, 1)
            dve.wait_ge(top_done, 2)
            nc.vector.tensor_copy(topf[:], topi[:]).then_inc(top_done, 1)
            dve.wait_ge(top_done, 3)
            iota_wide = iota[:].unsqueeze(1).to_broadcast([128, BATCH, EXPERTS])
            n = 3
            for k in range(TOPK):
                dst = chosen[:] if k == 0 else hit[:, k % 2]
                nc.vector.tensor_tensor(dst, iota_wide, topf[:, :, k:k + 1].to_broadcast([128, BATCH, EXPERTS]),
                                        ALU.is_equal).then_inc(top_done, 1)
                n += 1
                dve.wait_ge(top_done, n)
                if k:
                    nc.vector.tensor_tensor(chosen[:], chosen[:], hit[:, k % 2], ALU.add).then_inc(top_done, 1)
                    n += 1
                    dve.wait_ge(top_done, n)
            dve.wait_ge(exp_ready, 1)
            nc.vector.tensor_tensor(chosen[:], chosen[:], expl[:, :, 0:EXPERTS], ALU.mult).then_inc(top_done, 1)
            dve.wait_ge(top_done, n + 1)
            nc.vector.tensor_reduce(wsum[:], chosen[:], AX.X, ALU.add).then_inc(top_done, 1)
            dve.wait_ge(top_done, n + 2)
            nc.vector.reciprocal(wsum[:], wsum[:]).then_inc(top_done, 1)
            dve.wait_ge(top_done, n + 3)
            nc.vector.tensor_tensor(weight[:, :, 0:EXPERTS], chosen[:],
                                    wsum[:].unsqueeze(2).to_broadcast([128, BATCH, EXPERTS]), ALU.mult)
            nc.vector.tensor_scalar(expl[:, :, EXPERTS], expl[:, :, EXPERTS], 1.0, None, ALU.add).then_inc(top_done, 1)
            dve.wait_ge(top_done, n + 4)
            nc.vector.reciprocal(weight[:, :, EXPERTS], expl[:, :, EXPERTS]).then_inc(weight_ready, 1)

            def expert_step(b, q, live):
                first = not live(1)
                if first:
                    for e in range(UNITS):
                        dve.wait_ge(gu_hi_done, e + 1)
                        nc.vector.tensor_tensor(gu_lo[:, e], gu_raw[:, e], gu_hi[:, e].bitcast(F32),
                                                ALU.subtract).then_inc(gu_lo_done, 1)
                    dve.wait_ge(weight_ready, 1)
                    prepare(b, q)
                if live(0):
                    dve.wait_ge(xe_hi_done, b + 1)
                    for c in range(CH):
                        nc.vector.tensor_tensor(xe_lo[q][:, c, :], banks[7][:, c * 128:(c + 1) * 128],
                                                xe_hi[q][:, c, :].bitcast(F32), ALU.subtract).then_inc(xe_lo_done, 1)
                for e in range(UNITS):
                    if live(0):
                        dve.wait_ge(silu_ready, b * UNITS + e + 1)
                        at = weight[:, bass.ds(b, 1), min(e, EXPERTS):min(e, EXPERTS) + 1].rearrange("p a n -> p (a n)")
                        nc.vector.scalar_tensor_tensor(h_sb[:, e * INTER:(e + 1) * INTER], silu[e % 4][:], at,
                                                       banks[e % 4][:, INTER:2 * INTER], ALU.mult, ALU.mult).then_inc(h_ready, 1)
                    if e == 6 and live(1):
                        dve.wait_ge(down_used, b * FGRP)
                        xs = x[:, bass.ds(b - 1, 1), :].rearrange("p a n -> p (a n)")
                        nc.vector.tensor_tensor(xs, banks[6][:, 0:D], xs, ALU.add).then_inc(y_added, 1)
                    if e == 10 and live(0):
                        prepare_next(b, q)

            def prepare(b, q):
                normalise(xe[q][:], b, xe_ready)

            def prepare_next(b, q):
                prepare(b + 1, 1 - q)

            experts(expert_step, dve)



_INS = ["x", "wqkv", "bqk", "bv", "wo", "bo", "cos", "sin", "mask", "ident", "ctx", "skip", "kpad", "same", "turned", "gate",
        "gu", "down", "iota"]


def layouts(x, fside_S2_0, ctx_2048, L0_attn_W_Q, L0_attn_b_Q, L0_attn_W_K, L0_attn_b_K, L0_attn_W_V, L0_attn_b_V,
            L0_attn_W_O, L0_attn_b_O, L0_xattn_k, L0_ffn_gate_w, L0_ffn_expert_gate_up, L0_ffn_expert_down,
            L0_ffn_shared_gate_up, L0_ffn_shared_down, L0_ffn_shared_gate_vec):
    a = np.asarray
    def qk(w):
        return a(w).reshape(PAIRS, 2, CH, 128, 64, 2).transpose(0, 2, 3, 5, 1, 4).reshape(PAIRS, CH, 128, 256)
    wv = a(L0_attn_W_V).reshape(PAIRS, 2, CH, 128, DH).transpose(0, 2, 3, 1, 4).reshape(PAIRS, CH, 128, 256)
    wqkv = np.concatenate([qk(L0_attn_W_Q), qk(L0_attn_W_K), wv], axis=3)
    def bias(b):
        return a(b).reshape(PAIRS, 2, 64, 2).transpose(1, 2, 0, 3).reshape(128, PAIRS, 2)
    freqs = np.outer(np.arange(SEQ, dtype=np.float32),
                     (1.0 / np.float32(10000.0) ** (np.arange(0, DH, 2, dtype=np.float32) / DH)).astype(np.float32))
    gate = np.concatenate([a(L0_ffn_gate_w), a(L0_ffn_shared_gate_vec)])
    shared = a(L0_ffn_shared_gate_up).reshape(2, SHARED // INTER, INTER, D).transpose(1, 0, 2, 3)
    gu = np.concatenate([a(L0_ffn_expert_gate_up), shared.reshape(-1, 2 * INTER, D)])
    down = np.concatenate([a(L0_ffn_expert_down).transpose(0, 2, 1).reshape(-1, D), a(L0_ffn_shared_down).T])
    return {
        "x": a(x).transpose(1, 0, 2),
        "wqkv": wqkv,
        "bqk": np.concatenate([bias(L0_attn_b_Q), bias(L0_attn_b_K)], axis=2),
        "bv": a(L0_attn_b_V).T,
        "wo": a(L0_attn_W_O).transpose(1, 0, 2),
        "bo": a(L0_attn_b_O),
        "cos": np.tile(np.cos(freqs).T, (2, 1)).astype(np.float32),
        "sin": np.tile(np.sin(freqs).T, (2, 1)).astype(np.float32),
        "mask": np.where(np.tril(np.ones((SEQ, SEQ), bool)), 0.0, MASKED).astype(np.float32),
        "ident": np.eye(128, dtype=np.float32),
        "ctx": a(ctx_2048).transpose(1, 0, 2),
        "skip": a(fside_S2_0).reshape(SEQ, 1),
        "kpad": np.pad(a(L0_xattn_k), ((0, 0), (SEQ, 0))),
        "turned": np.eye(128, dtype=np.float32)[::-1],
        "same": np.kron(np.eye(FILTERS), np.ones((RANKS, RANKS))).astype(np.float32),
        "gate": gate.reshape(LG, CH, 128).transpose(2, 1, 0),
        "gu": gu.reshape(UNITS, 2 * INTER, CH, 128).transpose(3, 0, 2, 1),
        "down": down,
        "iota": np.tile(np.arange(EXPERTS, dtype=np.float32), (128, 1)),
    }

def kernel(**inputs):
    import concourse.bacc as bacc
    from concourse.bass_utils import run_bass_kernel_spmd

    laid_out = layouts(**inputs)
    nc = bacc.Bacc("TRN2", target_bir_lowering=False, num_devices=1)
    arrays, args = {}, []
    for name in _INS:
        array = np.ascontiguousarray(laid_out[name])
        arrays[f"in_{name}"] = array
        args.append(nc.dram_tensor(f"in_{name}", array.shape, mybir.dt.from_np(array.dtype), kind="ExternalInput").ap())
    out = nc.dram_tensor("out", (SEQ, BATCH, D), F32, kind="ExternalOutput").ap()
    decoder(nc, *args, out)
    done = run_bass_kernel_spmd(nc, [arrays], core_ids=[0])
    return done.results[0]["out"].transpose(1, 0, 2)
```

```python
import numpy as np
import concourse.bass as bass
from concourse import mybir
from contextlib import ExitStack

F32 = mybir.dt.float32
F32R = mybir.dt.float32r
ALU = mybir.AluOpType
ACT = mybir.ActivationFunctionType
AX = mybir.AxisListType

BATCH, SEQ, D = 16, 128, 256
HEADS, DH = 16, 128
PAIRS = HEADS // 2
GB = 4
GROUPS = BATCH // GB
GT = GB * SEQ
CH = D // 128
PW = 6 * 128
QE, QO, KE, KO, VV = 0, 128, 256, 384, 512
EPS = 1e-5
SCALE = float(DH) ** -0.5
MASKED = -1e30

RANKS = 8
FILTERS = SEQ // RANKS
HB = BATCH // 2

EXPERTS, TOPK, INTER, SHARED = 16, 4, 176, 704
UNITS = EXPERTS + SHARED // INTER
FEATS = UNITS * INTER
EARLY = 16
FCH = (FEATS + 127) // 128
FGRP = (FCH + 3) // 4
LOW_BYTES = 80 * 1024
LG = EXPERTS + 1


def decoder(nc, x_in, wqkv_in, bqk_in, bv_in, wo_in, bo_in, trig_in, mask_in, ident_in,
            ctx_in, skip_in, kpad_in, same_in, turned_in, gate_in, gu_in, down_in, iota_in, out):
    with ExitStack() as ctx:
        def sb(name, shape, dt=F32, c=ctx):
            return c.enter_context(nc.sbuf_tensor(name, shape, dt))

        def bank(name):
            return ctx.enter_context(nc.psum_tensor(name, [128, 512], F32))

        def sem(name):
            return ctx.enter_context(nc.semaphore(name))

        banks = [bank(f"bank{i}") for i in range(8)]

        x = sb("x", [128, BATCH + 1, D])
        ident = sb("ident", [128, 128])
        stats = sb("stats", [128, BATCH, 6])
        mv = sb("mv", [128, BATCH + 1, 2])
        rstd = sb("rstd", [128, BATCH + 1])
        var = sb("var", [128, BATCH])
        newton = sb("newton", [128, BATCH])
        warm = sb("warm", [128, 1])

        actx = ExitStack()
        xhat = sb("xhat", [128, GB, D], c=actx)
        xt_hi = sb("xt_hi", [128, CH, GT], F32R, actx)
        xt_lo = sb("xt_lo", [128, CH, GT], F32R, actx)
        raw = [sb(f"raw{i}", [128, PW], c=actx) for i in range(2)]
        w_hi = sb("w_hi", [128, PAIRS, CH, PW], F32R, actx)
        w_lo = sb("w_lo", [128, PAIRS, CH, PW], F32R, actx)
        wo = sb("wo", [128, HEADS, D], c=actx)
        bqk = sb("bqk", [128, PAIRS, 4], c=actx)
        bv = sb("bv", [128, HEADS], c=actx)
        bo = sb("bo", [128, D], c=actx)
        const = sb("const", [128, D], c=actx)
        trig = sb("trig", [128, 2, GB, SEQ], c=actx)
        mask = sb("mask", [128, SEQ], c=actx)
        turn_all = [sb(f"turn{m}", [128, 4, GT], c=actx) for m in range(2)]
        turn = [[t[:, i, :] for i in range(4)] for t in turn_all]
        rot = [[sb(f"rot{m}{h}", [128, GT], c=actx) for h in range(2)] for m in range(2)]
        v = [sb(f"v{i}", [128, GB, 2 * DH], c=actx) for i in range(2)]
        prob = [sb(f"prob{h}", [128, GB, SEQ], c=actx) for h in range(2)]
        prob_t = [sb(f"prob_t{h}", [128, GB, SEQ], c=actx) for h in range(2)]
        z_t = [sb(f"z_t{h}", [128, GB, SEQ], c=actx) for h in range(2)]
        negmax = sb("negmax", [128, 2, GB], c=actx)
        total = sb("total", [128, 2, GB], c=actx)
        rtotal = sb("rtotal", [128, 2, GB], c=actx)
        bv_wide = [*prob_t, *z_t]
        proj = banks[0:2]
        score = banks[2:4]
        pt_bank, zt_bank = banks[4], banks[5]
        qk_bank = [proj[0], proj[1], pt_bank, proj[0]]
        v_bank = [proj[1], pt_bank]
        acc = banks[6:8]

        actx.close()

        bctx = ExitStack()
        ctxg = [sb(f"ctxg{i}", [128, GB, D], c=bctx) for i in range(2)]
        xn = sb("xn", [128, GB, D], c=bctx)
        vcs = sb("vcs", [128, GB, D], c=bctx)
        v_t = sb("v_t", [128, CH, BATCH, SEQ], c=bctx)
        c_t = sb("c_t", [128, CH, BATCH, SEQ], c=bctx)
        o_t = sb("o_t", [128, CH, BATCH, SEQ], c=bctx)
        toep = [sb(f"toep{i}", [128, D], c=bctx) for i in range(2)]
        kv = [[sb(f"kv{i}{c}", [128, HB, RANKS, RANKS], c=bctx) for c in range(CH)] for i in range(2)]
        dc = kv
        zc = [sb(f"zc{c}", [128, HB, RANKS, RANKS], c=bctx) for c in range(CH)]
        skip = sb("skip", [128, 1], c=bctx)
        same = sb("same", [128, 128], c=bctx)
        turned = sb("turned", [128, 128], c=bctx)
        bctx.close()
        cctx = ExitStack()
        gu_hi = sb("gu_hi", [128, UNITS, CH, 2 * INTER], F32R, c=cctx)
        xg = sb("xg", [128, GB, D], c=cctx)
        xgt = sb("xgt", [128, CH, GT], c=cctx)
        logit = sb("logit", [128, BATCH, LG], c=cctx)
        top = sb("top", [128, BATCH, 8], c=cctx)
        topi = sb("topi", [128, BATCH, 8], mybir.dt.uint32, cctx)
        topf = sb("topf", [128, BATCH, 8], c=cctx)
        hit = sb("hit", [128, 2, BATCH, EXPERTS], c=cctx)
        chosen = sb("chosen", [128, BATCH, EXPERTS], c=cctx)
        expl = sb("expl", [128, BATCH, LG], c=cctx)
        wsum = sb("wsum", [128, BATCH], c=cctx)
        weight = sb("weight", [128, BATCH, LG], c=cctx)
        silu = [sb(f"silu{i}", [128, INTER], c=cctx) for i in range(4)]
        cctx.close()
        ectx = ExitStack()
        sb("below", [128, LOW_BYTES // 4], c=ectx)
        dctx = ExitStack()
        gu_raw = sb("gu_raw", [128, UNITS, CH, 2 * INTER], c=dctx)
        dctx.close()
        gu_lo = sb("gu_lo", [128, UNITS, CH, 2 * INTER], F32R, ectx)
        down = sb("down", [128, FCH, D], c=ectx)
        gate = sb("gate", [128, CH, LG], c=ectx)
        iota = sb("iota", [128, EXPERTS], c=ectx)
        dctx = ExitStack()
        toep_all = sb("toep_all", [128, FILTERS, D], c=dctx)
        dctx.close()
        h_sb = sb("h_sb", [128, FEATS], c=ectx)
        h_t = [sb(f"h_t{i}", [128, 4, 128], c=ectx) for i in range(2)]
        xe = [sb(f"xe{i}", [128, D], c=ectx) for i in range(2)]
        xe_hi = [sb(f"xe_hi{i}", [128, CH, 128], F32R, ectx) for i in range(2)]
        xe_lo = [sb(f"xe_lo{i}", [128, CH, 128], F32R, ectx) for i in range(2)]
        ectx.close()

        x_in_sem = [sem(f"x_loaded{g}") for g in range(GROUPS)]
        small_loaded = sem("small_loaded")
        wo_loaded = sem("wo_loaded")
        raw_loaded = [sem(f"raw_loaded{i}") for i in range(2)]
        w_hi_done = sem("w_hi_done")
        w_lo_done = sem("w_lo_done")
        spare_set = sem("spare_set")
        stats_done = sem("stats_done")
        var_ready = sem("var_ready")
        rstd_ready = sem("rstd_ready")
        newton_done = sem("newton_done")
        xhat_ready = sem("xhat_ready")
        xt_ready = sem("xt_ready")
        xt_hi_done = sem("xt_hi_done")
        xt_lo_done = sem("xt_lo_done")
        qk_ready = sem("qk_ready")
        qk_used = sem("qk_used")
        rot_dve = sem("rot_dve")
        rot_pool = sem("rot_pool")
        v_ready = sem("v_ready")
        v_taken = sem("v_taken")
        s_ready = sem("s_ready")
        s_taken = sem("s_taken")
        max_ready = sem("max_ready")
        exp_done = sem("exp_done")
        rtotal_ready = sem("rtotal_ready")
        prob_ready = [sem(f"prob_ready{h}") for h in range(2)]
        pt_ready = sem("pt_ready")
        pt_taken = sem("pt_taken")
        zt_ready = sem("zt_ready")
        zt_taken = sem("zt_taken")
        wo_done = sem("wo_done")
        acc_taken = sem("acc_taken")
        bv_spread = sem("bv_spread")
        const_summed = sem("const_summed")
        const_ready = sem("const_ready")
        const_added = sem("const_added")
        ctx_loaded = [sem(f"ctx_loaded{i}") for i in range(2)]
        conv_loaded = sem("conv_loaded")
        skip_loaded = sem("skip_loaded")
        gu_loaded = sem("gu_loaded")
        down_loaded = sem("down_loaded")
        xn_ready = sem("xn_ready")
        vcs_ready = sem("vcs_ready")
        vt_ready = sem("vt_ready")
        vt_taken = sem("vt_taken")
        ct_ready = sem("ct_ready")
        ct_taken = sem("ct_taken")
        skip_summed = sem("skip_summed")
        skip_taken = sem("skip_taken")
        skip_added = sem("skip_added")
        toep_turned = sem("toep_turned")
        toep_taken = sem("toep_taken")
        toep_ready = sem("toep_ready")
        kv_ready = sem("kv_ready")
        y_ready = sem("y_ready")
        y_taken = sem("y_taken")
        o_ready = sem("o_ready")
        back_ready = sem("back_ready")
        back_added = sem("back_added")
        gu_hi_done = sem("gu_hi_done")
        gu_lo_early = sem("gu_lo_early")
        gu_lo_late = sem("gu_lo_late")
        xg_ready = sem("xg_ready")
        xgt_ready = sem("xgt_ready")
        xgt_taken = sem("xgt_taken")
        logit_ready = sem("logit_ready")
        logit_taken = sem("logit_taken")
        shifted = sem("shifted")
        warmed = sem("warmed")
        top_done = sem("top_done")
        exp_ready = sem("exp_ready")
        weight_ready = sem("weight_ready")
        xe_ready = sem("xe_ready")
        xet_ready = sem("xet_ready")
        xe_hi_done = sem("xe_hi_done")
        xe_lo_done = sem("xe_lo_done")
        up_ready = sem("up_ready")
        silu_ready = sem("silu_ready")
        h_ready = sem("h_ready")
        ht_ready = sem("ht_ready")
        ht_taken = sem("ht_taken")
        down_used = sem("down_used")
        y_added = sem("y_added")
        stored = sem("stored")

        block = ctx.enter_context(nc.Block())

        def attention(step, eng):
            for p in range(PAIRS):
                step(0, p, lambda k, p=p: p >= k, True)
            with eng.Fori(1, GROUPS) as g:
                for p in range(PAIRS):
                    step(g, p, lambda k: True, False)
            for p in range(3):
                step(GROUPS, p, lambda k, p=p: p < k, False)

        @block.sync
        def _(sp):
            sp.dma_start(x[:, 0:GB, :], x_in[:, 0:GB, :]).then_inc(x_in_sem[0], 16)
            sp.dma_start(ident[:], ident_in).then_inc(small_loaded, 16)
            n = 0
            for p in range(PAIRS):
                for c in range(CH):
                    if n >= 2:
                        sp.wait_ge(w_hi_done, n - 1)
                        sp.wait_ge(w_lo_done, n - 1)
                    sp.dma_start(raw[n % 2][:], wqkv_in[p, c]).then_inc(raw_loaded[n % 2], 16)
                    n += 1
                if p == 0:
                    sp.dma_start(bqk[:], bqk_in).then_inc(small_loaded, 16)
                    sp.dma_start(trig[:], trig_in).then_inc(small_loaded, 16)
                    sp.dma_start(mask[:], mask_in).then_inc(small_loaded, 16)
                    sp.dma_start(bv[:], bv_in).then_inc(small_loaded, 16)
                    sp.dma_start(bo[:], bo_in.partition_broadcast(128)).then_inc(small_loaded, 16)
                    for g in range(1, GROUPS):
                        sp.dma_start(x[:, g * GB:(g + 1) * GB, :],
                                     x_in[:, g * GB:(g + 1) * GB, :]).then_inc(x_in_sem[g], 16)
                if p == 0:
                    sp.dma_start(wo[:], wo_in).then_inc(wo_loaded, 16)
            sp.wait_ge(v_ready, 2 * PAIRS * GROUPS)
            for g in range(2):
                sp.dma_start(ctxg[g][:], ctx_in[:, g * GB:(g + 1) * GB, :]).then_inc(ctx_loaded[g], 16)
            sp.wait_ge(acc_taken, 2 * GROUPS)
            sp.dma_start(skip[:], skip_in).then_inc(skip_loaded, 16)
            sp.dma_start(same[:], same_in).then_inc(skip_loaded, 16)
            sp.dma_start(turned[:], turned_in).then_inc(conv_loaded, 16)
            sp.dma_start(toep_all[:], bass.AP(tensor=kpad_in.tensor, offset=kpad_in.offset + 1,
                                              ap=[[1, 128], [SEQ + D, FILTERS], [1, D]])).then_inc(conv_loaded, 16)
            for g in range(2, GROUPS):
                sp.wait_ge(skip_taken, 2 * g - 2)
                sp.dma_start(ctxg[g % 2][:], ctx_in[:, g * GB:(g + 1) * GB, :]).then_inc(ctx_loaded[g % 2], 16)
            sp.dma_start(gate[:], gate_in).then_inc(gu_loaded, 16)
            sp.dma_start(iota[:], iota_in).then_inc(gu_loaded, 16)
            for part in range(4):
                u = slice(part * UNITS // 4, (part + 1) * UNITS // 4)
                sp.dma_start(gu_raw[:, u], gu_in[:, u]).then_inc(gu_loaded, 16)
            sp.dma_start(down[:, 0:FCH - 1, :], down_in[0:(FCH - 1) * 128].rearrange("(c p) n -> p c n", p=128)).then_inc(down_loaded, 16)
            sp.dma_start(down[0:FEATS - (FCH - 1) * 128, FCH - 1, :], down_in[(FCH - 1) * 128:FEATS]).then_inc(down_loaded, 16)
            with sp.Fori(0, BATCH) as b:
                sp.wait_ge(y_added, b + 1)
                sp.dma_start(out[:, bass.ds(b, 1), :], x[:, bass.ds(b, 1), :]).then_inc(stored, 16)
            sp.wait_ge(stored, 16 * BATCH)

        CONV = 2 * 16
        GU = 6 * 16

        def skip_term(i, j):
            return dc[i][j][:].rearrange("p b i j -> p (b i j)").rearrange("p (b l) -> p b l", b=2)

        def halves(step, eng):
            step(0, 0, True)
            step(1, 1, True)
            with eng.Fori(1, FILTERS // 2) as n:
                step(n * 2, 0, False)
                step(n * 2 + 1, 1, False)

        AHEAD = 12
        T_AT = [4, 7, 10, 13, 16, 19, 22]
        D_AT = [6, 9, 12, 15, 18, 21, 24]

        def experts(step, eng):
            step(0, 0, lambda k: k == 0)
            step(1, 1, lambda k: True)
            with eng.Fori(1, BATCH // 2) as n:
                step(n * 2, 0, lambda k: True)
                step(n * 2 + 1, 1, lambda k: True)
            step(BATCH, 0, lambda k: k == 1)

        SMALL = 6 * 16

        @block.tensor
        def _(pe):
            pe.wait_ge(small_loaded, SMALL)

            def product3(o, parts):
                n = len(parts)
                for i, (lh, ll, rh, rl) in enumerate(parts):
                    nc.tensor.matmul(o, lh, rh, start=(i == 0), stop=False)
                    nc.tensor.matmul(o, lh, rl, start=False, stop=False)
                    last = nc.tensor.matmul(o, ll, rh, start=False, stop=(i == n - 1))
                return last

            def project(p, col, o):
                return product3(o, [(w_hi[:, p, c, col:col + 128], w_lo[:, p, c, col:col + 128],
                                     xt_hi[:, c, :], xt_lo[:, c, :]) for c in range(CH)])

            def transpose_probs(s, h, live):
                pe.wait_ge(prob_ready[h], s - 1)
                if h == 0 and live(1):
                    pe.wait_ge(v_taken, s * 2)
                else:
                    pe.wait_ge(pt_taken, s * 2 - 4 + h)
                for b in range(GB):
                    last = nc.tensor.transpose(pt_bank[:, b * 128:(b + 1) * 128],
                                               prob[h][:, b, :], ident[:])
                last.then_inc(pt_ready, 1)

            def weigh_values(s, p, h, first):
                pe.wait_ge(pt_taken, s * 2 - 4 + h + 1)
                if not (first and p == 2 and h == 0):
                    pe.wait_ge(zt_taken, s * 2 - 4 + h)
                for b in range(GB):
                    last = nc.tensor.matmul(zt_bank[:, b * 128:(b + 1) * 128],
                                            v[p % 2][:, b, h * DH:(h + 1) * DH],
                                            prob_t[h][:, b, :], start=True, stop=True)
                last.then_inc(zt_ready, 1)

            def step(g, p, live, first):
                s = g * PAIRS + p
                if live(1):
                    q = (p - 1) % PAIRS
                    for half in range(2):
                        pe.wait_ge(qk_used, s * 4 - 2 + half)
                        for b in range(2):
                            t = (2 * half + b) * SEQ
                            last = product3(v_bank[half][:, b * 256:(b + 1) * 256],
                                            [(xt_hi[:, c, t:t + SEQ], xt_lo[:, c, t:t + SEQ],
                                              w_hi[:, q, c, VV:VV + 256], w_lo[:, q, c, VV:VV + 256])
                                             for c in range(CH)])
                        last.then_inc(v_ready, 1)
                if p == 0 and live(0):
                    pe.wait_ge(xhat_ready, g * GB + GB)
                    for c in range(CH):
                        if not first and c == 0:
                            pe.wait_ge(qk_used, s * 4)
                        if not first and c == 1:
                            pe.wait_ge(v_taken, s * 2 - 1)
                        for b in range(GB):
                            last = nc.tensor.transpose(proj[c][:, b * 128:(b + 1) * 128],
                                                       xhat[:, b, c * 128:(c + 1) * 128], ident[:])
                        last.then_inc(xt_ready, 1)
                if live(3):
                    r = (p - 3) % PAIRS
                    pe.wait_ge(zt_taken, s * 2 - 4)
                    if r == 0:
                        if first:
                            pe.wait_ge(const_ready, 1)
                        else:
                            pe.wait_ge(acc_taken, g * 2)
                    for b in range(GB):
                        for h in range(2):
                            last = nc.tensor.matmul(
                                acc[b // 2][:, (b % 2) * D:(b % 2 + 1) * D], z_t[h][:, b, :],
                                wo[:, 2 * r + h, :], start=(r == 0 and b % 2 == 0 and h == 0),
                                stop=(r == PAIRS - 1 and h == 1), skip_group_check=True)
                    last.then_inc(wo_done, 1)
                for h in range(2):
                    if live(2):
                        transpose_probs(s, h, live)
                        if h == 1:
                            weigh_values(s, p, 0, first)
                    if live(1):
                        if h == 0:
                            pe.wait_ge(rot_dve, s * 4)
                            pe.wait_ge(rot_pool, s * 4)
                        if live(2):
                            pe.wait_ge(s_taken, s * 2 - 4 + h + 1)
                        for b in range(GB):
                            t = slice(b * SEQ, (b + 1) * SEQ)
                            last = nc.tensor.matmul(score[h][:, t], rot[0][h][:, t], rot[1][h][:, t],
                                                    start=True, stop=True)
                        last.then_inc(s_ready, 1)
                if live(2):
                    weigh_values(s, p, 1, first)
                for i, col in enumerate((QE, QO, KE, KO)):
                    if live(0):
                        if first and i == 0:
                            pe.wait_ge(w_hi_done, 2 * p + 2)
                            pe.wait_ge(w_lo_done, 2 * p + 2)
                        if i == 0 and p == 0:
                            pe.wait_ge(xt_hi_done, g * 2 + 2)
                            pe.wait_ge(xt_lo_done, g * 2 + 2)
                        elif i == 0:
                            pe.wait_ge(qk_used, s * 4)
                        elif i == 1 and p > 0:
                            pe.wait_ge(v_taken, s * 2 - 1)
                        elif i == 2 and live(2):
                            pe.wait_ge(pt_taken, s * 2 - 2)
                        elif i == 2 and live(1):
                            pe.wait_ge(v_taken, s * 2)
                        elif i == 3:
                            pe.wait_ge(qk_used, s * 4 + 1)
                        project(p, col, qk_bank[i][:]).then_inc(qk_ready, 1)
                if first and p == 1:
                    pe.wait_ge(wo_loaded, 16)
                    pe.wait_ge(bv_spread, 4)
                    for n in range(HEADS):
                        last = nc.tensor.matmul(acc[0][:, 0:D], bv_wide[n // 4][:, n % 4, :], wo[:, n, :],
                                                start=(n == 0), stop=(n == HEADS - 1))
                    last.then_inc(const_summed, 1)

            attention(step, pe)

            pe.wait_ge(skip_loaded, 32)
            def turn_rows(n):
                pe.wait_ge(conv_loaded, CONV)
                for i in range(2):
                    if n:
                        pe.wait_ge(toep_taken, n * 2 - 1 + i)
                    f = n * 4 + 2 * i
                    nc.tensor.matmul(banks[6 + i][:], turned[:], toep_all[:, f:f + 2, :],
                                     start=True, stop=True).then_inc(toep_turned, 1)

            for g in range(GROUPS):
                pe.wait_ge(xn_ready, g * GB + GB)
                if g:
                    pe.wait_ge(vt_taken, g * 2)
                for c in range(CH):
                    for b in range(GB):
                        last = nc.tensor.transpose(banks[c][:, b * 128:(b + 1) * 128],
                                                   xn[:, b, c * 128:(c + 1) * 128], ident[:])
                    last.then_inc(vt_ready, 1)
                pe.wait_ge(ctx_loaded[g % 2], g // 2 * 16 + 16)
                if g:
                    pe.wait_ge(ct_taken, g * 2)
                for c in range(CH):
                    for b in range(GB):
                        last = nc.tensor.transpose(banks[2 + c][:, b * 128:(b + 1) * 128],
                                                   ctxg[g % 2][:, b, c * 128:(c + 1) * 128], ident[:])
                    last.then_inc(ct_ready, 1)
                pe.wait_ge(vcs_ready, g + 1)
                if g:
                    pe.wait_ge(skip_taken, g * 2)
                for j in range(2):
                    nc.tensor.matmul(banks[4 + j][:], same[:], vcs[:, 2 * j:2 * j + 2, :], start=True,
                                     stop=True).then_inc(skip_summed, 1)
                if g < GROUPS - 1:
                    turn_rows(g)
            pe.wait_ge(vt_taken, GROUPS * 2)
            pe.wait_ge(ct_taken, GROUPS * 2)

            for n in range(GROUPS - 1, FILTERS // 4):
                turn_rows(n)
            pe.wait_ge(toep_taken, FILTERS // 2)

            def conv_step(f, i, first):
                pe.wait_ge(toep_ready, f + 1)
                for half in range(2):
                    u = f * 2 + half
                    if not (first and i == 0):
                        pe.wait_ge(y_taken, u * 2 - 2)
                    pe.wait_ge(kv_ready, u * 2 + 1)
                    nc.tensor.matmul(banks[2 * half][:], toep[i][:, 0:128], kv[half][0][:],
                                     start=True, stop=True).then_inc(y_ready, 1)
                    pe.wait_ge(kv_ready, u * 2 + 2)
                    nc.tensor.matmul(banks[2 * half + 1][:], toep[i][:, 128:256], kv[half][0][:], start=True, stop=False)
                    nc.tensor.matmul(banks[2 * half + 1][:], toep[i][:, 0:128], kv[half][1][:],
                                     start=False, stop=True).then_inc(y_ready, 1)

            halves(conv_step, pe)

            pe.wait_ge(o_ready, 4 * FILTERS)
            pe.wait_ge(y_taken, 4 * FILTERS)
            for j in range(BATCH // 2):
                if j >= 4:
                    pe.wait_ge(back_added, j - 3)
                for b in range(2):
                    for c in range(CH):
                        last = nc.tensor.transpose(banks[4 + j % 4][:, (2 * b + c) * 128:(2 * b + c + 1) * 128],
                                                   o_t[:, c, 2 * j + b, :], ident[:])
                last.then_inc(back_ready, 1)

            pe.wait_ge(gu_loaded, GU)
            pe.wait_ge(back_added, BATCH // 2)
            def route(g, first):
                pe.wait_ge(xg_ready, g * GB + GB)
                for c in range(CH):
                    for b in range(GB):
                        last = nc.tensor.transpose(banks[c][:, b * 128:(b + 1) * 128],
                                                   xg[:, b, c * 128:(c + 1) * 128], ident[:])
                    last.then_inc(xgt_ready, 1)
                pe.wait_ge(xgt_taken, g * 2 + 2)
                if not first:
                    pe.wait_ge(logit_taken, g)
                for b in range(GB):
                    for c in range(CH):
                        last = nc.tensor.matmul(banks[2][:, b * LG:(b + 1) * LG],
                                                xgt[:, c, b * 128:(b + 1) * 128], gate[:, c, :],
                                                start=(c == 0), stop=(c == CH - 1), skip_group_check=True)
                last.then_inc(logit_ready, 1)

            route(0, True)
            with pe.Fori(1, GROUPS) as g:
                route(g, False)
            pe.wait_ge(logit_taken, GROUPS)

            def unit_up(b, q, e, first):
                if first:
                    pe.wait_ge(gu_hi_done, e + 1)
                    if e < EARLY:
                        pe.wait_ge(gu_lo_early, e + 1)
                    else:
                        pe.wait_ge(gu_lo_late, e - EARLY + 1)
                if not (first and e < 4):
                    pe.wait_ge(h_ready, b * UNITS + e - 3)
                product3(banks[e % 4][:, 0:2 * INTER],
                         [(xe_hi[q][:, c, :], xe_lo[q][:, c, :], gu_hi[:, e, c, :], gu_lo[:, e, c, :])
                          for c in range(CH)]).then_inc(up_ready, 1)

            def h_transposed(b, q, k, first):
                pe.wait_ge(h_ready, b * UNITS + min(UNITS, (512 * (k + 1) + INTER - 1) // INTER))
                n = b * FGRP + k
                if not (first and k < 2):
                    pe.wait_ge(ht_taken, n - 1)
                bank = banks[4 + (q * FGRP + k) % 2]
                for j in range(min(4, FCH - 4 * k)):
                    f = 128 * (4 * k + j)
                    w = min(128, FEATS - f)
                    last = nc.tensor.transpose(bank[0:w, j * 128:(j + 1) * 128], h_sb[:, f:f + w], ident[:])
                last.then_inc(ht_ready, 1)

            def h_down(b, q, k):
                pe.wait_ge(ht_taken, b * FGRP + k + 1)
                for j in range(min(4, FCH - 4 * k)):
                    c = 4 * k + j
                    w = min(128, FEATS - 128 * c)
                    last = nc.tensor.matmul(banks[6][:, 0:D], h_t[(q * FGRP + k) % 2][0:w, j, :], down[0:w, c, :],
                                            start=(c == 0), stop=(c == FCH - 1))
                last.then_inc(down_used, 1)


            def tile_transposed(b, q):
                pe.wait_ge(xe_ready, b + 1)
                for c in range(CH):
                    last = nc.tensor.transpose(banks[7][:, c * 128:(c + 1) * 128],
                                               xe[q][:, c * 128:(c + 1) * 128], ident[:])
                last.then_inc(xet_ready, 1)

            def expert_step(b, q, live):
                first = not live(1)
                if live(0):
                    if first:
                        tile_transposed(b, q)
                    pe.wait_ge(xe_hi_done, b + 1)
                    pe.wait_ge(xe_lo_done, b * 2 + 2)
                for e in range(UNITS):
                    if live(0):
                        unit_up(b, q, e, first)
                        if e == AHEAD:
                            tile_transposed(b + 1, 1 - q)
                    for k in range(FGRP):
                        if T_AT[k] == e and live(0):
                            h_transposed(b, q, k, first)
                        if T_AT[k] == e + UNITS and live(1):
                            h_transposed(b - 1, 1 - q, k, False)
                        if D_AT[k] == e and live(0):
                            if k == 0 and not first:
                                pe.wait_ge(y_added, b)
                            h_down(b, q, k)
                        if D_AT[k] == e + UNITS and live(1):
                            h_down(b - 1, 1 - q, k)

            pe.wait_ge(down_loaded, 32)
            experts(expert_step, pe)

        @block.scalar
        def _(act):
            def split_hi(n):
                act.wait_ge(raw_loaded[n % 2], 16 * (n // 2 + 1))
                nc.scalar.copy(w_hi[:, n // CH, n % CH, :], raw[n % 2][:]).then_inc(w_hi_done, 1)

            def root(k, lo, hi):
                act.wait_ge(var_ready, 2 * k + 2)
                nc.scalar.activation(rstd[:, lo:hi], newton[:, lo:hi], ACT.Sqrt).then_inc(rstd_ready, 1)

            root(0, 0, GB)
            split_hi(0)
            split_hi(1)

            def step(g, p, live, first):
                s = g * PAIRS + p

                def exps(h):
                    act.wait_ge(max_ready, s * 2 - 4 + h + 1)
                    for b in range(GB):
                        last = nc.scalar.activation(prob[h][:, b, :], prob[h][:, b, :], ACT.Exp,
                                                    bias=negmax[:, h, b:b + 1],
                                                    accum_out=total[:, h, b:b + 1])
                    last.then_inc(exp_done, 1)

                if first and p == 1:
                    root(1, GB, BATCH)
                for half in range(2):
                    if live(1):
                        act.wait_ge(v_ready, s * 2 - 2 + half + 1)
                        if live(3):
                            act.wait_ge(zt_ready, s * 2 - 4)
                        nc.scalar.copy(v[(p - 1) % 2][:, 2 * half:2 * half + 2, :],
                                       v_bank[half][:].rearrange("p (b n) -> p b n", b=2)).then_inc(v_taken, 1)
                    if half == 0 and live(2):
                        exps(0)
                if p == 0 and live(0):
                    for c in range(CH):
                        act.wait_ge(xt_ready, g * 2 + c + 1)
                        nc.scalar.copy(xt_hi[:, c, :], proj[c][:]).then_inc(xt_hi_done, 1)
                if live(2):
                    exps(1)
                if first and p < PAIRS - 1:
                    split_hi(2 * p + 2)
                    split_hi(2 * p + 3)
                if live(2):
                    for i in range(4):
                        h = i % 2
                        if i < 2:
                            act.wait_ge(pt_ready, s * 2 - 4 + h + 1)
                            if live(3):
                                act.wait_ge(zt_ready, s * 2 - 6 + h + 1)
                            nc.scalar.copy(prob_t[h][:], pt_bank[:].rearrange("p (b n) -> p b n", b=GB)).then_inc(pt_taken, 1)
                        else:
                            act.wait_ge(zt_ready, s * 2 - 4 + h + 1)
                            if live(3):
                                act.wait_ge(wo_done, s - 2)
                            nc.scalar.copy(z_t[h][:], zt_bank[:].rearrange("p (b n) -> p b n", b=GB)).then_inc(zt_taken, 1)

            attention(step, act)

            nc.scalar.activation(warm[:], ident[:, 0:1], ACT.Sqrt)
            root(2, 0, BATCH)
            def take_rows(n):
                for i in range(2):
                    act.wait_ge(toep_turned, n * 2 + i + 1)
                    f = n * 4 + 2 * i
                    nc.scalar.copy(toep_all[:, f:f + 2, :],
                                   banks[6 + i][:].rearrange("p (f l) -> p f l", f=2)).then_inc(toep_taken, 1)

            for g in range(GROUPS):
                for c in range(CH):
                    act.wait_ge(vt_ready, g * 2 + c + 1)
                    nc.scalar.copy(v_t[:, c, g * GB:(g + 1) * GB, :],
                                   banks[c][:].rearrange("p (b t) -> p b t", b=GB)).then_inc(vt_taken, 1)
                for c in range(CH):
                    act.wait_ge(ct_ready, g * 2 + c + 1)
                    nc.scalar.copy(c_t[:, c, g * GB:(g + 1) * GB, :],
                                   banks[2 + c][:].rearrange("p (b t) -> p b t", b=GB)).then_inc(ct_taken, 1)
                if g < GROUPS - 1:
                    take_rows(g)
            for n in range(GROUPS - 1, FILTERS // 4):
                take_rows(n)
            act.wait_ge(toep_taken, FILTERS // 2)

            def toep_step(f, i, first):
                if not first:
                    act.wait_ge(y_ready, f * 4 - 4)
                src = toep_all[:, i, :] if first else toep_all[:, bass.ds(f, 1), :].rearrange("p a n -> p (a n)")
                nc.scalar.copy(toep[i][:], src).then_inc(toep_ready, 1)

            halves(toep_step, act)


            act.wait_ge(back_ready, BATCH // 2)
            act.wait_ge(gu_loaded, GU)

            def split_units(units):
                for e in units:
                    nc.scalar.copy(gu_hi[:, e], gu_raw[:, e]).then_inc(gu_hi_done, 1)

            def x_high(b, q):
                act.wait_ge(xet_ready, b + 1)
                nc.scalar.copy(xe_hi[q][:], banks[7][:, 0:D].rearrange("p (c t) -> p c t", c=CH)).then_inc(xe_hi_done, 1)


            nc.scalar.activation(warm[:], ident[:, 0:1], ACT.Sqrt).then_inc(warmed, 1)
            split_units(range(0, EARLY // 2))
            root(3, 0, 2 * GB)
            split_units(range(EARLY // 2, UNITS))
            root(4, 2 * GB, BATCH)
            act.wait_ge(warmed, 1)
            nc.scalar.activation(warm[:], ident[:, 0:1], ACT.Exp)
            x_high(0, 0)
            act.wait_ge(shifted, 1)
            nc.scalar.activation(expl[:], expl[:], ACT.Exp).then_inc(exp_ready, 1)

            def expert_step(b, q, live):
                first = not live(1)
                for e in range(UNITS):
                    if e == AHEAD + 1 and live(0):
                        x_high(b + 1, 1 - q)
                    if live(0):
                        act.wait_ge(up_ready, b * UNITS + e + 1)
                        if not (first and e < 4):
                            act.wait_ge(h_ready, b * UNITS + e - 3)
                        nc.scalar.activation(silu[e % 4][:], banks[e % 4][:, 0:INTER], ACT.Silu).then_inc(silu_ready, 1)
                    for k in range(FGRP):
                        if T_AT[k] == e and live(0):
                            h_take(b, q, k, first)
                        if T_AT[k] == e + UNITS and live(1):
                            h_take(b - 1, 1 - q, k, False)

            def h_take(b, q, k, first):
                n = b * FGRP + k
                act.wait_ge(ht_ready, n + 1)
                if not (first and k < 2):
                    act.wait_ge(down_used, n - 1)
                i = (q * FGRP + k) % 2
                full = min(4, FEATS // 128 - 4 * k)
                src = banks[4 + i][:].rearrange("p (j t) -> p j t", j=4)
                if full == 4:
                    nc.scalar.copy(h_t[i][:], src).then_inc(ht_taken, 1)
                else:
                    w = FEATS % 128
                    nc.scalar.copy(h_t[i][:, 0:full, :], src[:, 0:full, :])
                    nc.scalar.copy(h_t[i][0:w, full, :], src[0:w, full, :]).then_inc(ht_taken, 1)

            experts(expert_step, act)

        @block.gpsimd
        def _(pool):
            nc.gpsimd.memset(x[:, BATCH, :], 0.0)
            nc.gpsimd.memset(mv[:, BATCH, :], 0.0)
            nc.gpsimd.memset(rstd[:, BATCH:BATCH + 1], 0.0).then_inc(spare_set, 1)
            pool.wait_ge(small_loaded, SMALL)
            for i in range(4):
                nc.gpsimd.tensor_copy(bv_wide[i][:],
                                      bv[:, 4 * i:4 * i + 4].unsqueeze(2).to_broadcast([128, 4, 128])).then_inc(bv_spread, 1)
            pool.wait_ge(bv_spread, 4)

            def step(g, p, live, first):
                s = g * PAIRS + p
                for m in range(2):
                    if live(0):
                        pool.wait_ge(qk_used, s * 4 + 2 * m + 2)
                        if live(1):
                            pool.wait_ge(s_ready, s * 2)
                        pool_rot(m, s)
                    if m == 1 and live(1):
                        pool.wait_ge(rtotal_ready, s * 2 - 1)
                        nc.gpsimd.tensor_tensor(prob[0][:], prob[0][:],
                                                rtotal[:, 0, :].unsqueeze(2).to_broadcast([128, GB, SEQ]),
                                                ALU.mult).then_inc(prob_ready[0], 1)
                        pool.wait_ge(prob_ready[0], s)
                if p == 5 and live(0):
                    pool.wait_ge(const_ready, 1)
                    pool.wait_ge(xhat_ready, g * GB + GB)
                    xg = x[:, 0:GB, :] if first else x[:, bass.ds(g * GB, GB), :]
                    nc.gpsimd.tensor_tensor(xg, xg, const[:].unsqueeze(1).to_broadcast([128, GB, D]),
                                            ALU.add).then_inc(const_added, 1)
                    pool.wait_ge(const_added, g + 1)

            def pool_rot(m, s):
                nc.gpsimd.tensor_tensor(rot[m][0][0:64, :], turn[m][0][0:64, :], turn[m][3][0:64, :],
                                        ALU.subtract).then_inc(rot_pool, 1)
                pool.wait_ge(rot_pool, s * 4 + 2 * m + 1)
                nc.gpsimd.tensor_tensor(rot[m][1][64:128, :], turn[m][1][64:128, :], turn[m][2][64:128, :],
                                        ALU.add).then_inc(rot_pool, 1)
                pool.wait_ge(rot_pool, s * 4 + 2 * m + 2)

            attention(step, pool)

            with pool.Fori(0, GROUPS // 2) as n:
                for i in range(2):
                    for j in range(2):
                        g = n * 2 + i
                        pool.wait_ge(skip_taken, g * 2 + j + 1)
                        xs = x[:, bass.ds(g * GB + 2 * j, 2), :]
                        nc.gpsimd.tensor_tensor(xs, xs, skip_term(i, j), ALU.add).then_inc(skip_added, 1)
            pool.wait_ge(vt_taken, 2 * GROUPS)
            pool.wait_ge(ct_taken, 2 * GROUPS)

            def kv_step(f, i, first):
                for half in range(2):
                    u = f * 2 + half
                    if not (first and i == 0):
                        pool.wait_ge(y_ready, u * 2 - 2)
                    ch = slice(i * RANKS, (i + 1) * RANKS) if first else bass.ds(f * RANKS, RANKS)
                    bs = slice(half * HB, (half + 1) * HB)
                    for c in range(CH):
                        nc.gpsimd.tensor_tensor(
                            kv[half][c][:],
                            v_t[:, c, bs, ch].unsqueeze(3).to_broadcast([128, HB, RANKS, RANKS]),
                            c_t[:, c, bs, ch].unsqueeze(2).to_broadcast([128, HB, RANKS, RANKS]),
                            ALU.mult).then_inc(kv_ready, 1)

            pool.wait_ge(skip_added, 2 * GROUPS)
            halves(kv_step, pool)

            for e in range(EARLY):
                pool.wait_ge(gu_hi_done, e + 1)
                nc.gpsimd.tensor_tensor(gu_lo[:, e], gu_raw[:, e], gu_hi[:, e].bitcast(F32),
                                        ALU.subtract).then_inc(gu_lo_early, 1)

        @block.vector
        def _(dve):
            counts = [0]

            def token_stats(k, lo, hi, early=0):
                done = counts[0]
                for b in range(max(lo, early), hi):
                    if k < 2:
                        dve.wait_ge(x_in_sem[b // GB], 16)
                    nc.vector.bn_stats(stats[:, b, :], x[:, b, :]).then_inc(stats_done, 1)
                for b in range(lo, hi):
                    dve.wait_ge(stats_done, done + b - lo + 1)
                    last = nc.vector.bn_aggr(mv[:, b, :], stats[:, b, :])
                last.then_inc(stats_done, 1)
                counts[0] = done + hi - lo + 1
                dve.wait_ge(stats_done, counts[0])
                r, v, n = rstd[:, lo:hi], var[:, lo:hi], newton[:, lo:hi]
                nc.vector.tensor_scalar(v, mv[:, lo:hi, 1], EPS, None, ALU.add).then_inc(var_ready, 1)
                dve.wait_ge(var_ready, 2 * k + 1)
                nc.vector.reciprocal(n, v).then_inc(var_ready, 1)
                dve.wait_ge(rstd_ready, k + 1)
                nc.vector.tensor_tensor(n, r, r, ALU.mult).then_inc(newton_done, 1)
                dve.wait_ge(newton_done, 4 * k + 1)
                nc.vector.tensor_tensor(n, n, v, ALU.mult).then_inc(newton_done, 1)
                dve.wait_ge(newton_done, 4 * k + 2)
                nc.vector.tensor_scalar(n, n, -0.5, 1.5, ALU.mult, ALU.add).then_inc(newton_done, 1)
                dve.wait_ge(newton_done, 4 * k + 3)
                nc.vector.tensor_tensor(r, r, n, ALU.mult).then_inc(newton_done, 1)
                dve.wait_ge(newton_done, 4 * k + 4)

            def normalise(dst, b, done):
                nc.vector.tensor_scalar(dst, x[:, bass.ds(b, 1), :].rearrange("p a n -> p (a n)"),
                                        mv[:, bass.ds(b, 1), 0:1].rearrange("p a n -> p (a n)"),
                                        rstd[:, bass.ds(b, 1)], ALU.subtract, ALU.mult).then_inc(done, 1)

            token_stats(0, 0, GB)
            dve.wait_ge(small_loaded, SMALL)

            def split_lo(n):
                dve.wait_ge(w_hi_done, n + 1)
                nc.vector.tensor_tensor(w_lo[:, n // CH, n % CH, :], raw[n % 2][:],
                                        w_hi[:, n // CH, n % CH, :].bitcast(F32), ALU.subtract).then_inc(w_lo_done, 1)

            def step(g, p, live, first):
                s = g * PAIRS + p
                if p == 0 and live(0):
                    for c in range(CH):
                        dve.wait_ge(xt_hi_done, g * 2 + c + 1)
                        nc.vector.tensor_tensor(xt_lo[:, c, :], proj[c][:], xt_hi[:, c, :].bitcast(F32),
                                                ALU.subtract).then_inc(xt_lo_done, 1)
                    if first:
                        split_lo(0)
                        split_lo(1)
                if first and p == 1:
                    token_stats(1, GB, BATCH)
                if not live(0) and p == 1:
                    dve.wait_ge(acc_taken, 2 * GROUPS - 2)
                    for b in range(BATCH - GB):
                        nc.vector.bn_stats(stats[:, b, :], x[:, b, :]).then_inc(stats_done, 1)
                if first and p < PAIRS - 1:
                    split_lo(2 * p + 2)
                    split_lo(2 * p + 3)
                if p == PAIRS - 1 and live(0):
                    dve.wait_ge(xt_ready, g * 2 + 2)
                    ahead = (g + 1) % GROUPS
                    for b in range(GB):
                        normalise(xhat[:, b, :], ahead * GB + b, xhat_ready)
                for m in range(2):
                    t = turn[m]
                    if live(0):
                        for i in range(2):
                            dve.wait_ge(qk_ready, s * 4 + 2 * m + i + 1)
                            if i == 0 and live(1):
                                dve.wait_ge(rot_pool, s * 4 - 2 + 2 * m)
                                dve.wait_ge(rot_dve, s * 4 - 2 + 2 * m)
                            last = nc.vector.scalar_tensor_tensor(
                                turn_all[m][:, 2 * i:2 * i + 2, :], qk_bank[2 * m + i][:].unsqueeze(1).to_broadcast([128, 2, GT]),
                                bqk[:, p, 2 * m + i:2 * m + i + 1],
                                trig[:].rearrange("p a b t -> p a (b t)"), ALU.add, ALU.mult)
                            last.then_inc(qk_used, 1)
                if live(1):
                    for h in range(2):
                        dve.wait_ge(s_ready, s * 2 - 2 + h + 1)
                        nc.vector.scalar_tensor_tensor(
                            prob[h][:], score[h][:].rearrange("p (b t) -> p b t", b=GB), SCALE,
                            mask[:].unsqueeze(1).to_broadcast([128, GB, SEQ]), ALU.mult, ALU.add).then_inc(s_taken, 1)
                        dve.wait_ge(s_taken, s * 2 - 2 + h + 1)
                        nc.vector.tensor_reduce(negmax[:, h, :], prob[h][:], AX.X, ALU.max, negate=True).then_inc(max_ready, 1)
                if p == 2 and live(3):
                    for i in range(2):
                        dve.wait_ge(wo_done, g * PAIRS)
                        dve.wait_ge(const_added, g)
                        xs = x[:, bass.ds(g * GB - GB + 2 * i, 2), :]
                        nc.vector.tensor_tensor(xs, acc[i][:].rearrange("p (b n) -> p b n", b=2), xs,
                                                ALU.add).then_inc(acc_taken, 1)

                def totals(h):
                    dve.wait_ge(exp_done, s * 2 - 2 + h + 1)
                    nc.vector.reciprocal(rtotal[:, h, :], total[:, h, :]).then_inc(rtotal_ready, 1)

                for m in range(2):
                    t = turn[m]
                    if live(0):
                        dve.wait_ge(qk_used, s * 4 + 2 * m + 2)
                        if live(1):
                            dve.wait_ge(s_ready, s * 2)
                        nc.vector.tensor_tensor(rot[m][1][0:64, :], t[0][64:128, :], t[3][64:128, :],
                                                ALU.subtract).then_inc(rot_dve, 1)
                    if m == 0 and live(1):
                        totals(0)
                    if live(0):
                        nc.vector.tensor_tensor(rot[m][0][64:128, :], t[1][0:64, :], t[2][0:64, :],
                                                ALU.add).then_inc(rot_dve, 1)
                if live(1):
                    totals(1)
                    dve.wait_ge(rtotal_ready, s * 2)
                    nc.vector.tensor_tensor(prob[1][:], prob[1][:],
                                            rtotal[:, 1, :].unsqueeze(2).to_broadcast([128, GB, SEQ]),
                                            ALU.mult).then_inc(prob_ready[1], 1)
                if first and p == 1:
                    dve.wait_ge(const_summed, 1)
                    nc.vector.tensor_tensor(const[:], acc[0][:, 0:D], bo[:], ALU.add).then_inc(const_ready, 1)

            for b in range(GB):
                normalise(xhat[:, b, :], b, xhat_ready)
            attention(step, dve)

            dve.wait_ge(acc_taken, 2 * GROUPS)
            token_stats(2, 0, BATCH, early=BATCH - GB)
            dve.wait_ge(skip_loaded, 32)
            for b in range(GB):
                normalise(xn[:, b, :], b, xn_ready)
            for g in range(GROUPS):
                dve.wait_ge(xn_ready, g * GB + GB)
                dve.wait_ge(ctx_loaded[g % 2], g // 2 * 16 + 16)
                if g:
                    dve.wait_ge(skip_summed, g * 2)
                nc.vector.scalar_tensor_tensor(vcs[:], xn[:], skip[:], ctxg[g % 2][:], ALU.mult, ALU.mult).then_inc(vcs_ready, 1)
                if g < GROUPS - 1:
                    dve.wait_ge(vt_ready, g * 2 + 2)
                    dve.wait_ge(vcs_ready, g + 1)
                    for b in range(GB):
                        normalise(xn[:, b, :], (g + 1) * GB + b, xn_ready)
                for j in range(2):
                    dve.wait_ge(skip_summed, g * 2 + j + 1)
                    if g > 1:
                        dve.wait_ge(skip_added, g * 2 + j - 3)
                    nc.vector.tensor_tensor(skip_term(g % 2, j), banks[4 + j][:].rearrange("p (b n) -> p b n", b=2),
                                            ctxg[g % 2][:, 2 * j:2 * j + 2, :], ALU.mult).then_inc(skip_taken, 1)

            def z_step(f, i, first):
                for half in range(2):
                    u = f * 2 + half
                    ch = slice(i * RANKS, (i + 1) * RANKS) if first else bass.ds(f * RANKS, RANKS)
                    bs = slice(half * HB, (half + 1) * HB)
                    for c in range(CH):
                        dve.wait_ge(y_ready, u * 2 + c + 1)
                        if not (first and i == 0 and half == 0):
                            dve.wait_ge(o_ready, u * 2 - 2 + c + 1)
                        nc.vector.tensor_tensor(
                            zc[c][:], banks[2 * half + c][:].rearrange("p (b i j) -> p b i j", b=HB, i=RANKS),
                            c_t[:, c, bs, ch].unsqueeze(3).to_broadcast([128, HB, RANKS, RANKS]),
                            ALU.mult).then_inc(y_taken, 1)
                    for c in range(CH):
                        dve.wait_ge(y_taken, u * 2 + c + 1)
                        nc.vector.tensor_reduce(o_t[:, c, bs, ch], zc[c][:].rearrange("p b i j -> p b j i"),
                                                AX.X, ALU.add).then_inc(o_ready, 1)

            halves(z_step, dve)
            dve.wait_ge(skip_added, 2 * GROUPS)
            for j in range(BATCH // 2):
                dve.wait_ge(back_ready, j + 1)
                xs = x[:, 2 * j:2 * j + 2, :]
                nc.vector.tensor_tensor(xs, banks[4 + j % 4][:].rearrange("p (b n) -> p b n", b=2), xs,
                                        ALU.add).then_inc(back_added, 1)

            def low(b, q):
                dve.wait_ge(xe_hi_done, b + 1)
                for c in range(CH):
                    nc.vector.tensor_tensor(xe_lo[q][:, c, :], banks[7][:, c * 128:(c + 1) * 128],
                                            xe_hi[q][:, c, :].bitcast(F32), ALU.subtract).then_inc(xe_lo_done, 1)

            def prepare(b, q):
                normalise(xe[q][:], b, xe_ready)

            dve.wait_ge(back_added, BATCH // 2)
            token_stats(3, 0, 2 * GB)

            def route(g, first, more):
                for c in range(CH):
                    dve.wait_ge(xgt_ready, g * 2 + c + 1)
                    nc.vector.tensor_copy(xgt[:, c, :], banks[c][:]).then_inc(xgt_taken, 1)
                if more:
                    for b in range(GB):
                        normalise(xg[:, b, :], (g + 1) * GB + b, xg_ready)
                    if first:
                        token_stats(4, 2 * GB, BATCH)
                else:
                    prepare(0, 0)
                dve.wait_ge(logit_ready, g + 1)
                nc.vector.tensor_copy(logit[:, bass.ds(g * GB, GB), :],
                                      banks[2][:, 0:GB * LG].rearrange("p (b e) -> p b e", b=GB)).then_inc(logit_taken, 1)

            for b in range(GB):
                normalise(xg[:, b, :], b, xg_ready)
            route(0, True, True)
            with dve.Fori(1, GROUPS - 1) as g:
                route(g, False, True)
            route(GROUPS - 1, False, False)
            dve.wait_ge(gu_loaded, GU)
            dve.wait_ge(logit_taken, GROUPS)
            for b in range(BATCH):
                last = nc.vector.max(top[:, b, :], logit[:, b, 0:EXPERTS])
            last.then_inc(top_done, 1)
            dve.wait_ge(top_done, 1)
            nc.vector.tensor_tensor(expl[:, :, 0:EXPERTS], logit[:, :, 0:EXPERTS],
                                    top[:, :, 0:1].to_broadcast([128, BATCH, EXPERTS]), ALU.subtract)
            nc.vector.tensor_scalar(expl[:, :, EXPERTS], logit[:, :, EXPERTS], -1.0, None, ALU.mult).then_inc(shifted, 1)
            low(0, 0)
            for b in range(BATCH):
                last = nc.vector.max_index(topi[:, b, :], top[:, b, :], logit[:, b, 0:EXPERTS])
            last.then_inc(top_done, 1)
            dve.wait_ge(top_done, 2)
            nc.vector.tensor_copy(topf[:], topi[:]).then_inc(top_done, 1)
            dve.wait_ge(top_done, 3)
            iota_wide = iota[:].unsqueeze(1).to_broadcast([128, BATCH, EXPERTS])
            n = 3
            for k in range(TOPK):
                dst = chosen[:] if k == 0 else hit[:, k % 2]
                nc.vector.tensor_tensor(dst, iota_wide, topf[:, :, k:k + 1].to_broadcast([128, BATCH, EXPERTS]),
                                        ALU.is_equal).then_inc(top_done, 1)
                n += 1
                dve.wait_ge(top_done, n)
                if k:
                    nc.vector.tensor_tensor(chosen[:], chosen[:], hit[:, k % 2], ALU.add).then_inc(top_done, 1)
                    n += 1
                    dve.wait_ge(top_done, n)
            dve.wait_ge(exp_ready, 1)
            nc.vector.tensor_tensor(chosen[:], chosen[:], expl[:, :, 0:EXPERTS], ALU.mult).then_inc(top_done, 1)
            dve.wait_ge(top_done, n + 1)
            nc.vector.tensor_reduce(wsum[:], chosen[:], AX.X, ALU.add).then_inc(top_done, 1)
            dve.wait_ge(top_done, n + 2)
            nc.vector.reciprocal(wsum[:], wsum[:]).then_inc(top_done, 1)
            dve.wait_ge(top_done, n + 3)
            nc.vector.tensor_tensor(weight[:, :, 0:EXPERTS], chosen[:],
                                    wsum[:].unsqueeze(2).to_broadcast([128, BATCH, EXPERTS]), ALU.mult)
            nc.vector.tensor_scalar(expl[:, :, EXPERTS], expl[:, :, EXPERTS], 1.0, None, ALU.add).then_inc(top_done, 1)
            dve.wait_ge(top_done, n + 4)
            nc.vector.reciprocal(weight[:, :, EXPERTS], expl[:, :, EXPERTS]).then_inc(weight_ready, 1)

            def expert_step(b, q, live):
                first = not live(1)
                if first:
                    dve.wait_ge(weight_ready, 1)
                for e in range(UNITS):
                    if e == AHEAD + 2 and live(0):
                        low(b + 1, 1 - q)
                    if live(0):
                        dve.wait_ge(silu_ready, b * UNITS + e + 1)
                        at = weight[:, bass.ds(b, 1), min(e, EXPERTS):min(e, EXPERTS) + 1].rearrange("p a n -> p (a n)")
                        nc.vector.scalar_tensor_tensor(h_sb[:, e * INTER:(e + 1) * INTER], silu[e % 4][:], at,
                                                       banks[e % 4][:, INTER:2 * INTER], ALU.mult, ALU.mult).then_inc(h_ready, 1)
                    if first and EARLY + e < UNITS:
                        late = EARLY + e
                        dve.wait_ge(gu_hi_done, late + 1)
                        nc.vector.tensor_tensor(gu_lo[:, late], gu_raw[:, late], gu_hi[:, late].bitcast(F32),
                                                ALU.subtract).then_inc(gu_lo_late, 1)
                    if e == 6 and live(1):
                        dve.wait_ge(down_used, b * FGRP)
                        xs = x[:, bass.ds(b - 1, 1), :].rearrange("p a n -> p (a n)")
                        nc.vector.tensor_tensor(xs, banks[6][:, 0:D], xs, ALU.add).then_inc(y_added, 1)
                    if e == 8 and live(0):
                        prepare_next(b, q)

            def prepare_next(b, q):
                prepare(b + 1, 1 - q)

            experts(expert_step, dve)



_INS = ["x", "wqkv", "bqk", "bv", "wo", "bo", "trig", "mask", "ident", "ctx", "skip", "kpad", "same", "turned", "gate",
        "gu", "down", "iota"]


def layouts(x, fside_S2_0, ctx_2048, L0_attn_W_Q, L0_attn_b_Q, L0_attn_W_K, L0_attn_b_K, L0_attn_W_V, L0_attn_b_V,
            L0_attn_W_O, L0_attn_b_O, L0_xattn_k, L0_ffn_gate_w, L0_ffn_expert_gate_up, L0_ffn_expert_down,
            L0_ffn_shared_gate_up, L0_ffn_shared_down, L0_ffn_shared_gate_vec):
    a = np.asarray
    def qk(w):
        return a(w).reshape(PAIRS, 2, CH, 128, 64, 2).transpose(0, 2, 3, 5, 1, 4).reshape(PAIRS, CH, 128, 256)
    wv = a(L0_attn_W_V).reshape(PAIRS, 2, CH, 128, DH).transpose(0, 2, 3, 1, 4).reshape(PAIRS, CH, 128, 256)
    wqkv = np.concatenate([qk(L0_attn_W_Q), qk(L0_attn_W_K), wv], axis=3)
    def bias(b):
        return a(b).reshape(PAIRS, 2, 64, 2).transpose(1, 2, 0, 3).reshape(128, PAIRS, 2)
    freqs = np.outer(np.arange(SEQ, dtype=np.float32),
                     (1.0 / np.float32(10000.0) ** (np.arange(0, DH, 2, dtype=np.float32) / DH)).astype(np.float32))
    gate = np.concatenate([a(L0_ffn_gate_w), a(L0_ffn_shared_gate_vec)])
    shared = a(L0_ffn_shared_gate_up).reshape(2, SHARED // INTER, INTER, D).transpose(1, 0, 2, 3)
    gu = np.concatenate([a(L0_ffn_expert_gate_up), shared.reshape(-1, 2 * INTER, D)])
    down = np.concatenate([a(L0_ffn_expert_down).transpose(0, 2, 1).reshape(-1, D), a(L0_ffn_shared_down).T])
    return {
        "x": a(x).transpose(1, 0, 2),
        "wqkv": wqkv,
        "bqk": np.concatenate([bias(L0_attn_b_Q), bias(L0_attn_b_K)], axis=2),
        "bv": a(L0_attn_b_V).T,
        "wo": a(L0_attn_W_O).transpose(1, 0, 2),
        "bo": a(L0_attn_b_O),
        "trig": np.tile(np.stack([np.cos(freqs).T, np.sin(freqs).T], 1)[:, :, None, :], (2, 1, GB, 1)).astype(np.float32),
        "mask": np.where(np.tril(np.ones((SEQ, SEQ), bool)), 0.0, MASKED).astype(np.float32),
        "ident": np.eye(128, dtype=np.float32),
        "ctx": a(ctx_2048).transpose(1, 0, 2),
        "skip": a(fside_S2_0).reshape(SEQ, 1),
        "kpad": np.pad(a(L0_xattn_k), ((0, 0), (SEQ, 0))),
        "turned": np.eye(128, dtype=np.float32)[::-1],
        "same": np.kron(np.eye(FILTERS), np.ones((RANKS, RANKS))).astype(np.float32),
        "gate": gate.reshape(LG, CH, 128).transpose(2, 1, 0),
        "gu": gu.reshape(UNITS, 2 * INTER, CH, 128).transpose(3, 0, 2, 1),
        "down": down,
        "iota": np.tile(np.arange(EXPERTS, dtype=np.float32), (128, 1)),
    }

def kernel(**inputs):
    import concourse.bacc as bacc
    from concourse.bass_utils import run_bass_kernel_spmd

    laid_out = layouts(**inputs)
    nc = bacc.Bacc("TRN2", target_bir_lowering=False, num_devices=1)
    arrays, args = {}, []
    for name in _INS:
        array = np.ascontiguousarray(laid_out[name])
        arrays[f"in_{name}"] = array
        args.append(nc.dram_tensor(f"in_{name}", array.shape, mybir.dt.from_np(array.dtype), kind="ExternalInput").ap())
    out = nc.dram_tensor("out", (SEQ, BATCH, D), F32, kind="ExternalOutput").ap()
    decoder(nc, *args, out)
    done = run_bass_kernel_spmd(nc, [arrays], core_ids=[0])
    return done.results[0]["out"].transpose(1, 0, 2)
```
